# Optimizing a Trainium2 kernel written in Bass

```python
import numpy as np
import jax
import jax.numpy as jnp

def _softmax(x, axis=-1):
    return jax.nn.softmax(x, axis=axis)

def _gelu(x):
    return jax.nn.gelu(x, approximate=True)

def _silu(x):
    return jax.nn.silu(x)

def _sigmoid(x):
    return jax.nn.sigmoid(x)

def _layernorm(x, axis=-1, eps=1e-05):
    m = jnp.mean(x, axis=axis, keepdims=True)
    v = jnp.var(x, axis=axis, keepdims=True)
    return (x - m) / jnp.sqrt(v + eps)

def _scatter_add(tgt, idx, src, axis=0):
    return tgt.at[idx].add(src)

def _segment_sum(src, seg, n):
    return jax.ops.segment_sum(src, seg, n)
kernel_name = 'mk_conv_preact_d2_conv_nhwc1024_r4_c8eeff'

def setup_inputs(seed: int=0):
    np.random.seed(seed)
    _w = jnp.asarray

    def _rec_inputs():
        import jax
        import jax.numpy as jnp
        _gk = jax.random.key(seed)
        x = -0.000125 + 0.9999 * jax.random.normal(jax.random.fold_in(_gk, 1), (32, 16, 16, 256), jnp.float32)
        return x
    x = _rec_inputs()

    def _L0_conv_setup():
        import math
        import jax, jax.numpy as jnp
        import numpy as np
        WIN = 8
        SHIFT = 4
        HEADS = 16
        LOG100 = math.log(100.0)

        def _rel_position_index(wh, ww):
            ch, cw = np.meshgrid(np.arange(wh), np.arange(ww), indexing='ij')
            coords = np.stack([ch.ravel(), cw.ravel()])
            rel = (coords[:, :, None] - coords[:, None, :]).transpose(1, 2, 0)
            rel[:, :, 0] += wh - 1
            rel[:, :, 1] += ww - 1
            rel[:, :, 0] *= 2 * ww - 1
            return rel.sum(-1).ravel()

        def _coords_table(wh, ww):
            rh = np.arange(-(wh - 1), wh, dtype=np.float32)
            rw = np.arange(-(ww - 1), ww, dtype=np.float32)
            t = np.stack(np.meshgrid(rh, rw, indexing='ij'), axis=-1)[None]
            t[..., 0] /= wh - 1
            t[..., 1] /= ww - 1
            t *= 8.0
            return np.sign(t) * np.log2(np.abs(t) + 1.0) / 3.0

        def _shift_mask(H, W, win, shift):
            m = np.zeros((H, W), np.int32)
            cnt = 0
            for hs in ((0, -win), (-win, -shift), (-shift, None)):
                for ws in ((0, -win), (-win, -shift), (-shift, None)):
                    m[hs[0]:hs[1], ws[0]:ws[1]] = cnt
                    cnt += 1
            nW = H // win * (W // win)
            m = m.reshape(H // win, win, W // win, win).transpose(0, 2, 1, 3).reshape(nW, win * win)
            return m[:, None, :] != m[:, :, None]
        key = jax.random.key(seed)
        ks = jax.random.split(key, 11)
        D, HID = (256, 128)
        s = 0.02
        return {'x': jax.random.normal(ks[0], (32, 16, 16, D), jnp.float32), 'Wq': jax.random.normal(ks[1], (D, D), jnp.float32) * s, 'Wk': jax.random.normal(ks[2], (D, D), jnp.float32) * s, 'Wv': jax.random.normal(ks[3], (D, D), jnp.float32) * s, 'bv': jax.random.normal(ks[4], (D,), jnp.float32) * s, 'Wo': jax.random.normal(ks[5], (D, D), jnp.float32) * s, 'bo': jax.random.normal(ks[6], (D,), jnp.float32) * s, 'logit_scale': jnp.full((HEADS, 1, 1), jnp.log(10.0), jnp.float32), 'cpb_w1': jax.random.normal(ks[7], (HID, 2), jnp.float32) * 0.5, 'cpb_b1': jax.random.normal(ks[8], (HID,), jnp.float32) * 0.1, 'cpb_w2': jax.random.normal(ks[9], (HEADS, HID), jnp.float32) * 0.1}
    _L0_conv_all = _L0_conv_setup()
    _L0_conv_in = {k: v for k, v in _L0_conv_all.items() if k in ('Wq', 'Wk', 'Wv', 'bv', 'Wo', 'bo', 'logit_scale', 'cpb_w1', 'cpb_b1', 'cpb_w2')}
    del _L0_conv_all

    def _L1_conv_setup():
        import jax, jax.numpy as jnp
        import numpy as np
        HEADS = 16

        def _self_attention(x, w_qkv, w_out, heads):
            b, t, d = x.shape
            dh = d // heads
            qkv = x @ w_qkv
            q, k, v = jnp.split(qkv, 3, axis=-1)
            split = lambda z: z.reshape(b, t, heads, dh).transpose(0, 2, 1, 3)
            q, k, v = (split(q), split(k), split(v))
            dots = jnp.einsum('bhie,bhje->bhij', q, k) * d ** (-0.5)
            out = jnp.einsum('bhij,bhje->bhie', dots, v)
            out = out.transpose(0, 2, 1, 3).reshape(b, t, d)
            return out @ w_out
        key = jax.random.key(seed)
        ks = jax.random.split(key, 5)
        B, H, W, D = (8, 16, 16, 256)
        s = D ** (-0.5)
        return {'x': jax.random.normal(ks[0], (B, H, W, D), jnp.float32), 'w_qkv0': jax.random.normal(ks[1], (D, 3 * D), jnp.float32) * s, 'w_out0': jax.random.normal(ks[2], (D, D), jnp.float32) * s, 'w_qkv1': jax.random.normal(ks[3], (D, 3 * D), jnp.float32) * s, 'w_out1': jax.random.normal(ks[4], (D, D), jnp.float32) * s}
    _L1_conv_all = _L1_conv_setup()
    _L1_conv_in = {k: v for k, v in _L1_conv_all.items() if k in ('w_qkv0', 'w_out0', 'w_qkv1', 'w_out1')}
    del _L1_conv_all
    return {'x': x, 'L0_conv_Wq': _L0_conv_in['Wq'], 'L0_conv_Wk': _L0_conv_in['Wk'], 'L0_conv_Wv': _L0_conv_in['Wv'], 'L0_conv_bv': _L0_conv_in['bv'], 'L0_conv_Wo': _L0_conv_in['Wo'], 'L0_conv_bo': _L0_conv_in['bo'], 'L0_conv_logit_scale': _L0_conv_in['logit_scale'], 'L0_conv_cpb_w1': _L0_conv_in['cpb_w1'], 'L0_conv_cpb_b1': _L0_conv_in['cpb_b1'], 'L0_conv_cpb_w2': _L0_conv_in['cpb_w2'], 'L1_conv_w_qkv0': _L1_conv_in['w_qkv0'], 'L1_conv_w_out0': _L1_conv_in['w_out0'], 'L1_conv_w_qkv1': _L1_conv_in['w_qkv1'], 'L1_conv_w_out1': _L1_conv_in['w_out1']}

def reference(x, L0_conv_Wq, L0_conv_Wk, L0_conv_Wv, L0_conv_bv, L0_conv_Wo, L0_conv_bo, L0_conv_logit_scale, L0_conv_cpb_w1, L0_conv_cpb_b1, L0_conv_cpb_w2, L1_conv_w_qkv0, L1_conv_w_out0, L1_conv_w_qkv1, L1_conv_w_out1):
    import jax
    import jax.numpy as jnp

    def _L0_conv_ref(x, Wq, Wk, Wv, bv, Wo, bo, logit_scale, cpb_w1, cpb_b1, cpb_w2):
        import math
        import jax, jax.numpy as jnp
        import numpy as np
        WIN = 8
        SHIFT = 4
        HEADS = 16
        LOG100 = math.log(100.0)

        def _rel_position_index(wh, ww):
            ch, cw = np.meshgrid(np.arange(wh), np.arange(ww), indexing='ij')
            coords = np.stack([ch.ravel(), cw.ravel()])
            rel = (coords[:, :, None] - coords[:, None, :]).transpose(1, 2, 0)
            rel[:, :, 0] += wh - 1
            rel[:, :, 1] += ww - 1
            rel[:, :, 0] *= 2 * ww - 1
            return rel.sum(-1).ravel()

        def _coords_table(wh, ww):
            rh = np.arange(-(wh - 1), wh, dtype=np.float32)
            rw = np.arange(-(ww - 1), ww, dtype=np.float32)
            t = np.stack(np.meshgrid(rh, rw, indexing='ij'), axis=-1)[None]
            t[..., 0] /= wh - 1
            t[..., 1] /= ww - 1
            t *= 8.0
            return np.sign(t) * np.log2(np.abs(t) + 1.0) / 3.0

        def _shift_mask(H, W, win, shift):
            m = np.zeros((H, W), np.int32)
            cnt = 0
            for hs in ((0, -win), (-win, -shift), (-shift, None)):
                for ws in ((0, -win), (-win, -shift), (-shift, None)):
                    m[hs[0]:hs[1], ws[0]:ws[1]] = cnt
                    cnt += 1
            nW = H // win * (W // win)
            m = m.reshape(H // win, win, W // win, win).transpose(0, 2, 1, 3).reshape(nW, win * win)
            return m[:, None, :] != m[:, :, None]
        B, H, W, D = x.shape
        N = WIN * WIN
        d = D // HEADS
        nWh, nWw = (H // WIN, W // WIN)
        nW = nWh * nWw
        xs = jnp.roll(x, (-SHIFT, -SHIFT), axis=(1, 2))
        xw = xs.reshape(B, nWh, WIN, nWw, WIN, D).transpose(0, 1, 3, 2, 4, 5)
        xw = xw.reshape(B * nW, N, D)
        q = (xw @ Wq.T).reshape(-1, N, HEADS, d).transpose(0, 2, 1, 3)
        k = (xw @ Wk.T).reshape(-1, N, HEADS, d).transpose(0, 2, 1, 3)
        v = (xw @ Wv.T + bv).reshape(-1, N, HEADS, d).transpose(0, 2, 1, 3)
        qn = q / jnp.maximum(jnp.linalg.norm(q, axis=-1, keepdims=True), 1e-12)
        kn = k / jnp.maximum(jnp.linalg.norm(k, axis=-1, keepdims=True), 1e-12)
        scale = jnp.exp(jnp.minimum(logit_scale, LOG100))
        logits = jnp.einsum('bhnd,bhmd->bhnm', qn, kn) * scale
        table = jnp.asarray(_coords_table(WIN, WIN))
        hcpb = jax.nn.relu(table @ cpb_w1.T + cpb_b1) @ cpb_w2.T
        tab = hcpb.reshape(-1, HEADS)
        idx = jnp.asarray(_rel_position_index(WIN, WIN))
        bias = tab[idx].reshape(N, N, HEADS).transpose(2, 0, 1)[None]
        logits = logits + 16.0 * jax.nn.sigmoid(bias)
        mask = jnp.asarray(_shift_mask(H, W, WIN, SHIFT))
        lg = logits.reshape(B, nW, HEADS, N, N)
        lg = jnp.where(mask[None, :, None], -jnp.inf, lg)
        logits = lg.reshape(B * nW, HEADS, N, N)
        scores = jax.nn.softmax(logits, axis=-1)
        o = jnp.einsum('bhnm,bhmd->bhnd', scores, v)
        o = o.transpose(0, 2, 1, 3).reshape(B * nW, N, D)
        z = o @ Wo.T + bo
        z = z.reshape(B, nWh, nWw, WIN, WIN, D).transpose(0, 1, 3, 2, 4, 5).reshape(B, H, W, D)
        return jnp.roll(z, (SHIFT, SHIFT), axis=(1, 2))

    def _L1_conv_ref(x, w_qkv0, w_out0, w_qkv1, w_out1):
        import jax, jax.numpy as jnp
        import numpy as np
        HEADS = 16

        def _self_attention(x, w_qkv, w_out, heads):
            b, t, d = x.shape
            dh = d // heads
            qkv = x @ w_qkv
            q, k, v = jnp.split(qkv, 3, axis=-1)
            split = lambda z: z.reshape(b, t, heads, dh).transpose(0, 2, 1, 3)
            q, k, v = (split(q), split(k), split(v))
            dots = jnp.einsum('bhie,bhje->bhij', q, k) * d ** (-0.5)
            out = jnp.einsum('bhij,bhje->bhie', dots, v)
            out = out.transpose(0, 2, 1, 3).reshape(b, t, d)
            return out @ w_out
        b, hh, ww, d = x.shape
        xh = x.transpose(0, 2, 1, 3).reshape(b * ww, hh, d)
        oh = _self_attention(xh, w_qkv0, w_out0, HEADS)
        oh = oh.reshape(b, ww, hh, d).transpose(0, 2, 1, 3)
        xw = x.reshape(b * hh, ww, d)
        ow = _self_attention(xw, w_qkv1, w_out1, HEADS)
        ow = ow.reshape(b, hh, ww, d)
        return oh + ow

    def _gn(v, G=32, eps=1e-05):
        B_, H_, W_, C_ = v.shape
        g = v.reshape(B_, H_, W_, G, C_ // G)
        m = jnp.mean(g, axis=(1, 2, 4), keepdims=True)
        s = jnp.var(g, axis=(1, 2, 4), keepdims=True)
        return ((g - m) / jnp.sqrt(s + eps)).reshape(v.shape)

    def _ln_c(v, eps=1e-06):
        m = jnp.mean(v, axis=-1, keepdims=True)
        s = jnp.var(v, axis=-1, keepdims=True)
        return (v - m) / jnp.sqrt(s + eps)

    def _ln_t(v, eps=1e-05):
        m = jnp.mean(v, axis=-1, keepdims=True)
        s = jnp.var(v, axis=-1, keepdims=True)
        return (v - m) / jnp.sqrt(s + eps)

    def _to_tokens(v):
        B_, H_, W_, C_ = v.shape
        return v.reshape(B_, H_ * W_, C_)

    def _from_tokens(t, like):
        return t.reshape(like.shape)
    x = x + _L0_conv_ref(_gn(x), L0_conv_Wq, L0_conv_Wk, L0_conv_Wv, L0_conv_bv, L0_conv_Wo, L0_conv_bo, L0_conv_logit_scale, L0_conv_cpb_w1, L0_conv_cpb_b1, L0_conv_cpb_w2)
    x = x + _L1_conv_ref(_gn(x), L1_conv_w_qkv0, L1_conv_w_out0, L1_conv_w_qkv1, L1_conv_w_out1)
    return x

_drawn_inputs = setup_inputs


def setup_inputs(seed=0):
    import zlib

    import numpy as np

    out = dict(_drawn_inputs(seed))
    spreads = {'L0_conv_logit_scale': (2.3025851249694824, 0.2)}
    factors = {'L0_conv_bv': 6.102, 'L0_conv_cpb_b1': 7.776}
    for name, (base, spread) in spreads.items():
        noise = np.random.default_rng([zlib.crc32(name.encode()), seed]).standard_normal(out[name].shape)
        drawn = base * np.exp(spread * noise) if base else spread * noise
        out[name] = jnp.asarray(drawn.astype(out[name].dtype))
    for name, factor in factors.items():
        out[name] = (out[name] * factor).astype(out[name].dtype)
    return out
```

```python
from collections import namedtuple
from contextlib import ExitStack

import numpy as np

import concourse.bass as bass
from concourse import mybir

ALU = mybir.AluOpType
ACT = mybir.ActivationFunctionType
F32 = mybir.dt.float32
F16 = mybir.dt.float16

P = 128
IMAGES, SIDE, D = 32, 16, 256
TOK = SIDE * SIDE
G = D // P
HEADS, DH = 16, 16
PAIRS = HEADS // 2
WIN, SHIFT = 8, 4
N = WIN * WIN
NW = TOK // N
SEQ = SIDE
BLOCKS = TOK // 32
REL = 2 * WIN - 1
REACH = (WIN - 1) * REL + WIN
WS = 64.0
GS = 2.0 ** -4
HALF = G * TOK
LOG100 = float(np.log(100.0))
NORM_MIN = 1e-12
QS = 8.0 * WS
LN_BIAS = 2.0 ** -63
SAFE_SCALE = 72.0
MASKED = -1.0e30
GN_EPS = 1e-5
PASSES = ((0, 0), (1, 0), (0, 1))

Image = namedtuple("Image", "n par half")


def image(i, c):
    return Image(2 * i + c, c % 2, i + c // 2)


def previous(img):
    return Image(img.n - 1, 1 - img.par, None)


def missing(n):
    return isinstance(n, int) and n < 0


def reach(eng, sem, img, per=1, j=None):
    if not missing(img.n):
        eng.wait_ge(sem, img.n * per + (per if j is None else j))


def constants():
    p = np.arange(P)
    ident = np.eye(P, dtype=np.float32)
    group = ((p[:, None] // 8 == p[None, :] // 8) / 16.0).astype(np.float32)
    heads = (p[:, None] // DH == p[None, :] // DH).astype(np.float32)
    halves = (p[:, None] // 64 == np.arange(32)[None, :] // DH).astype(np.float32)
    quad = (p[:, None] // 32 == np.arange(4)[None, :]).astype(np.float32)
    odd = ((p[:, None] // 16) % 2 == np.arange(2)[None, :]).astype(np.float32)
    eighth = (p[:, None] // 16 == np.arange(8)[None, :]).astype(np.float32)
    odd_g = odd * np.float32(GS / (WS * WS))
    extra = np.zeros((P, 8), np.float32)
    extra[:, 0], extra[:, 1], extra[:, 2], extra[:, 3] = LN_BIAS, np.log(8.0), -0.5, -0.5
    small = np.concatenate([halves, quad, odd, eighth, odd_g, extra], 1)
    region = np.digitize(np.arange(SIDE), [SIDE - WIN, SIDE - SHIFT])
    label = (3 * region[:, None] + region[None, :]).reshape(2, WIN, 2, WIN).transpose(0, 2, 1, 3).reshape(NW, N)
    mask = np.where(label[:, None, :] != label[:, :, None], np.float32(MASKED), np.float32(0))
    mask = np.tile(mask.transpose(2, 0, 1), (2, 1, 1)).reshape(P, NW * N).astype(np.float32)
    at = np.arange(-(WIN - 1), WIN, dtype=np.float32) / (WIN - 1) * 8.0
    at = (np.sign(at) * np.log2(np.abs(at) + 1.0) / 3.0).astype(np.float32)
    coords = np.stack(np.meshgrid(at[::-1], at[::-1], indexing="ij")).reshape(2, REL * REL).astype(np.float32)
    return {"c_ident": ident, "c_group": group, "c_heads": heads, "c_small": small, "c_mask": mask, "c_coords": coords}


def build(nc, x, Wq, Wk, Wv, bv, Wo, bo, logit_scale, cpb_w1, cpb_b1, cpb_w2, w_qkv0, w_out0, w_qkv1, w_out1,
          c_ident, c_group, c_heads, c_small, c_mask, c_coords, out, scratch):
    ctx = ExitStack()
    with ctx:
        def sb(name, shape, dt=F32):
            return ctx.enter_context(nc.sbuf_tensor(name, shape, dt))

        def sem(name):
            return ctx.enter_context(nc.semaphore(name))

        ident = sb("ident", [P, P])
        group8 = sb("group8", [P, P])
        head16 = sb("head16", [P, P])
        small = sb("small", [P, 56])
        ones_pair = small[:, 0:32]
        quad_mask = small[:, 32:36]
        odd_mask = small[:, 36:38]
        head_mask = small[:, 38:46]
        odd_mask_g = small[:, 46:48]
        ln_bias = small[:, 48:49]
        ln8 = small[:, 49:50]
        minus_half = small[:, 50:52]
        bo_col = sb("bo_col", [P, G])
        bv_rows = sb("bv_rows", [P, G, D])
        q_ln = sb("q_ln", [P, G])
        q_cap = sb("q_cap", [P, G])
        bias_mask = sb("bias_mask", [P, PAIRS, NW, N])
        w_l0 = {m: sb(f"w_{m}", [P, 2, 2, D], F16) for m in "qkvo"}
        w_l1 = [{m: sb(f"w{a}_{m}", [P, 2, 2, D], F16) for m in "qkvo"} for a in range(2)]
        x_in = sb("x_in", [P, 2, 2, D])
        x_t = sb("x_t", [P, 2, HALF])
        stat = [sb(f"stat{l}", [P, 44]) for l in range(2)]
        xn32 = [sb(f"xn32_{l}", [P, HALF]) for l in range(2)]
        xn = [sb(f"xn{l}", [P, 2, HALF], F16) for l in range(2)]
        qk_sq = sb("qk_sq", [P, 2, HALF])
        qk32 = sb("qk32", [P, 2, HALF])
        qk = sb("qk", [P, 2, 2, G, TOK], F16)
        k_heads = sb("k_heads", [P, 2, G, NW, 8, N], F16)
        v_diag = sb("v_diag", [P, 2, 2, PAIRS, 32])
        probs = sb("probs", [P, PAIRS, TOK])
        den_inv = sb("den_inv", [P, HALF])
        o32 = sb("o32", [P, HALF])
        o = sb("o", [P, 2, HALF], F16)
        z = sb("z", [P, HALF])
        x1 = sb("x1", [P, 2, HALF])
        q1 = [sb(f"q1_{a}", [P, 2, HALF], F16) for a in range(2)]
        kv32 = sb("kv32", [P, 2, HALF])
        kv = [sb(f"kv_{a}", [P, 2, 2, HALF], F16) for a in range(2)]
        k_wide = [sb(f"k_wide{a}", [P, 2, G * BLOCKS, 4, 32], F16) for a in range(2)]
        v_wide = [sb(f"v_wide{a}", [P, 2, G * BLOCKS, 2, 32], F16) for a in range(2)]
        gram_t = sb("gram_t", [P, HALF])
        gram32 = sb("gram32", [P, HALF])
        gram = [sb(f"gram{a}", [P, 2, HALF], F16) for a in range(2)]
        gram_wide = [sb(f"gram_wide{a}", [P, 2, G * SEQ, 8, 16], F16) for a in range(2)]
        o1 = [sb(f"o1_{a}", [P, 2, HALF], F16) for a in range(2)]
        y = sb("y", [P, HALF])
        y_out = sb("y_out", [P, 2, 2, D])
        ps = ctx.enter_context(nc.psum_tensor("ps", [P, 8, 512], F32))

        consts_in = sem("consts_in")
        weights_in = sem("weights_in")
        table_step = sem("table_step")
        hidden_done = sem("hidden_done")
        hidden_relu = sem("hidden_relu")
        table_done = sem("table_done")
        table_exp = sem("table_exp")
        scale_exp = sem("scale_exp")
        q_cap_exp = sem("q_cap_exp")
        tables_ready = sem("tables_ready")
        w_turned = sem("w_turned")
        w_hi = sem("w_hi")
        w_lo = sem("w_lo")
        zeroed = sem("zeroed")
        table_out = sem("table_out")
        table_in = sem("table_in")
        x_loaded = [sem(f"x_loaded{p}") for p in range(2)]
        xt_done = sem("xt_done")
        xt_copied = sem("xt_copied")
        gn_small = [sem(f"gn_small{l}") for l in range(2)]
        gn_sum = [sem(f"gn_sum{l}") for l in range(2)]
        gn_pow = [sem(f"gn_pow{l}") for l in range(2)]
        xn_hi = [sem(f"xn_hi{l}") for l in range(2)]
        xn_lo = [sem(f"xn_lo{l}") for l in range(2)]
        qk_proj = sem("qk_proj")
        v_proj = sem("v_proj")
        qk_squared = sem("qk_squared")
        norms_done = sem("norms_done")
        ln_done = sem("ln_done")
        rnorm_done = sem("rnorm_done")
        qk_scaled = sem("qk_scaled")
        qk_hi = sem("qk_hi")
        qk_lo = sem("qk_lo")
        k_masked = sem("k_masked")
        v_ready = sem("v_ready")
        scores_done = sem("scores_done")
        biased = sem("biased")
        probs_ready = sem("probs_ready")
        den_done = sem("den_done")
        pv_done = sem("pv_done")
        den_inverted = sem("den_inverted")
        o_scaled = sem("o_scaled")
        o_hi = sem("o_hi")
        o_lo = sem("o_lo")
        z_proj = sem("z_proj")
        z_ready = sem("z_ready")
        x1_ready = sem("x1_ready")
        kv1_proj = [sem(f"kv1_proj{a}") for a in range(2)]
        q1_proj = [sem(f"q1_proj{a}") for a in range(2)]
        kv_turned = [sem(f"kv_turned{a}") for a in range(2)]
        kv_hi = [sem(f"kv_hi{a}") for a in range(2)]
        kv_lo = [sem(f"kv_lo{a}") for a in range(2)]
        q1_hi = [sem(f"q1_hi{a}") for a in range(2)]
        q1_lo = [sem(f"q1_lo{a}") for a in range(2)]
        kv_widened = [sem(f"kv_widened{a}") for a in range(2)]
        gram_done = [sem(f"gram_done{a}") for a in range(2)]
        gram_even = [sem(f"gram_even{a}") for a in range(2)]
        gram_summed = [sem(f"gram_summed{a}") for a in range(2)]
        gram_hi = [sem(f"gram_hi{a}") for a in range(2)]
        gram_lo = [sem(f"gram_lo{a}") for a in range(2)]
        widened_dve = [sem(f"widened_dve{a}") for a in range(2)]
        widened_act = [sem(f"widened_act{a}") for a in range(2)]
        o1_done = [sem(f"o1_done{a}") for a in range(2)]
        o1_hi = [sem(f"o1_hi{a}") for a in range(2)]
        o1_lo = [sem(f"o1_lo{a}") for a in range(2)]
        y_proj = sem("y_proj")
        y_added = sem("y_added")
        yt_done = sem("yt_done")
        y_copied = sem("y_copied")
        stored = [sem(f"stored{p}") for p in range(2)]

        GN_STEPS = 11
        ACT_HEADS = 2

        stage_l0 = {"q": qk32[:, 0, :], "k": qk32[:, 1, :], "v": qk_sq[:, 0, :], "o": qk_sq[:, 1, :]}
        stage_qkv = [probs[:, 0:6, :].rearrange("p a b -> p (a b)").rearrange("p (c n) -> p c n", c=2),
                     gram_wide[0][:].rearrange("p t s h e -> p (t s h e)").bitcast(F32)[:, 0:6 * D].rearrange(
                         "p (c n) -> p c n", c=2)]
        stage_out = [kv32[:, 0, :].rearrange("p (c n) -> p c n", c=2),
                     kv32[:, 1, :].rearrange("p (c n) -> p c n", c=2)]
        mask_in = sb("mask_in", [P, NW, N])
        table_rows = z[:, :]
        reach_in = sb("reach_in", [P, PAIRS, REL * WIN])
        coords = sb("coords", [2, REL * REL])
        w1_t = sb("w1_t", [2, P])
        b1_col = sb("b1_col", [P, 1])
        w2_t = sb("w2_t", [P, HEADS])
        scale_col = sb("scale_col", [HEADS, 8])
        table = sb("table", [HEADS, 3, REL * REL])
        N_CONST = 19 + 16

        def windows(ap):
            return ap.rearrange("p (a b i j) -> p a b i j", b=2, i=WIN, j=WIN)

        def raster(ap, c=SIDE):
            return ap.rearrange("p (r c) -> p r c", c=c)

        def along(ap, a):
            v = ap.rearrange("p (g r c) -> p g r c", r=SIDE, c=SIDE)
            return v.rearrange("p g r c -> p g c r") if a == 0 else v

        def in_seq(ap):
            return ap.rearrange("p (g s i) -> p g s i", s=SEQ, i=SEQ)

        x_rows = x.rearrange("n r c d -> n (r c) d")
        out_rows = out.rearrange("n r c d -> n (r c) d")

        def pieces(rows, buf):
            s = SHIFT * SIDE
            return [(buf[:, 0, :], rows[s:s + P]), (buf[0:64, 1, :], rows[s + P:TOK]), (buf[64:P, 1, :], rows[0:s])]

        block = ctx.enter_context(nc.Block())

        def over_steps(eng, step):
            for k in (-1, 0, 1):
                step(0, k, load=True, l0=k >= 0, l1=k >= 1, ahead=True)
            with eng.Fori(0, (IMAGES - 4) // 2) as i:
                for u in range(2):
                    step(i, 2 + u, load=True, l0=True, l1=True, ahead=True)
            for k in (IMAGES - 2, IMAGES - 1, IMAGES):
                step(0, k, load=False, l0=k < IMAGES, l1=True, ahead=k < IMAGES - 1)

        @block.sync
        def _(sp):
            n = [0]

            def const(dst, src, **kw):
                n[0] += 1
                sp.dma_start(dst, src, **kw).then_inc(consts_in, 16)

            const(ident[:], c_ident)
            const(group8[:], c_group)
            const(head16[:], c_heads)
            const(small[:], c_small)
            const(mask_in[:].rearrange("p w n -> p (w n)"), c_mask)
            const(coords[:], c_coords)
            const(w1_t[:], cpb_w1.rearrange("h c -> c h"), allow_slow_non_contiguous=True)
            const(b1_col[:], cpb_b1.rearrange("(h a) -> h a", a=1))
            const(w2_t[:], cpb_w2.rearrange("h m -> m h"), allow_slow_non_contiguous=True)
            const(scale_col[:, 0:1], logit_scale.rearrange("h a b -> h (a b)"))
            const(bo_col[:], bo.rearrange("(g p) -> p g", p=P), allow_slow_non_contiguous=True)
            for h in range(8):
                const(q_ln[DH * h:DH * h + DH, :],
                      bass.AP(logit_scale.tensor, h, [[0, DH], [8, G], [1, 1]]), allow_slow_non_contiguous=True)
            for t in range(2):
                for rows in range(8):
                    const(bv_rows[16 * rows:16 * rows + 16, t, :], bass.AP(bv.tensor, 0, [[0, 16], [1, D]]))
            assert n[0] == N_CONST
            for m, w in (("q", Wq), ("k", Wk), ("v", Wv), ("o", Wo)):
                sp.dma_start(stage_l0[m].rearrange("p (a n) -> p a n", a=2),
                             w.rearrange("(a p) n -> p a n", p=P)).then_inc(weights_in, 16)
            for a, (wi, wo) in enumerate(((w_qkv0, w_out0), (w_qkv1, w_out1))):
                sp.dma_start(stage_qkv[a], wi.rearrange("(a p) n -> p a n", p=P)).then_inc(weights_in, 16)
                sp.dma_start(stage_out[a], wo.rearrange("(a p) n -> p a n", p=P)).then_inc(weights_in, 16)
            for b in range(2):
                for dst, src in pieces(x_rows[b], x_in[:, b]):
                    sp.dma_start(dst, src).then_inc(x_loaded[b], 16)
            sp.wait_ge(table_step, 6)
            sp.dma_start(scratch, table[:, 2, :]).then_inc(table_out, 16)
            sp.wait_ge(table_out, 16)
            for b in range(2):
                for mi in range(WIN):
                    src = bass.AP(scratch.tensor, b * REL * REL + mi * REL,
                                  [[1, WIN], [2 * REL * REL, PAIRS], [1, REACH]])
                    sp.dma_start(reach_in[64 * b + 8 * mi:64 * b + 8 * mi + 8, :, 0:REACH], src).then_inc(table_in, 16)

            def step(i, c, load, l0, l1, ahead):
                now, before, after2 = image(i, c), image(i, c - 1), image(i, c + 2)
                if load and c >= 0:
                    reach(sp, xt_done, now)
                    for dst, src in pieces(x_rows[after2.n], x_in[:, after2.par]):
                        sp.dma_start(dst, src).then_inc(x_loaded[after2.par], 16)
                if l1:
                    reach(sp, y_copied, before)
                    for src, dst in pieces(out_rows[before.n], y_out[:, before.par]):
                        sp.dma_start(dst, src).then_inc(stored[before.par], 16)

            over_steps(sp, step)
            for b in range(2):
                sp.wait_ge(stored[b], 48 * (IMAGES // 2))

        @block.tensor
        def _(pe):
            pe.wait_ge(consts_in, 16 * N_CONST)
            pe.matmul(ps[:, 0, 0:REL * REL], w1_t[:], coords[:], start=True, stop=True).then_inc(hidden_done, 1)
            pe.wait_ge(hidden_relu, 1)
            pe.matmul(ps[0:HEADS, 1, 0:REL * REL], w2_t[:], table_rows[:, 0:REL * REL],
                      start=True, stop=True).then_inc(table_done, 1)
            pe.wait_ge(weights_in, 16 * 8)
            for t, m in enumerate("qkvo"):
                for a in range(2):
                    for c in range(2):
                        last = pe.transpose(ps[:, 2 + t, c * D + a * P:c * D + a * P + P],
                                            stage_l0[m][:, a * D + c * P:a * D + c * P + P], ident[:])
                last.then_inc(w_turned, 1)

            def project(dst, w, act, m):
                n = 0
                for c in range(2):
                    for wp, xp in PASSES:
                        last = pe.matmul(dst, w[:, wp, c, m * P:m * P + P], act[:, xp, c * TOK:(c + 1) * TOK],
                                         start=(n == 0), stop=(n == 5))
                        n += 1
                return last

            def axial_proj(a, before):
                for t, m in enumerate("kv"):
                    for g in range(G):
                        last = project(ps[:, 3 + t, g * TOK:(g + 1) * TOK], w_l1[a][m], xn[1], g)
                last.then_inc(kv1_proj[a], 1)
                if a == 1:
                    reach(pe, q1_lo[0], before)
                for g in range(G):
                    last = project(ps[:, 5, g * TOK:(g + 1) * TOK], w_l1[a]["q"], xn[1], g)
                last.then_inc(q1_proj[a], 1)

            def gram_matmuls(a, before):
                reach(pe, kv_widened[a], before)
                for s in range(G * BLOCKS):
                    dst = ps[:, 6 + s // 8, (s % 8) * 64:(s % 8) * 64 + 64]
                    for n, (kp, vp) in enumerate(PASSES):
                        last = pe.matmul(dst, k_wide[a][:, kp, s].rearrange("p q e -> p (q e)"),
                                         v_wide[a][:, vp, s].rearrange("p q e -> p (q e)"),
                                         start=(n == 0), stop=(n == 2))
                last.then_inc(gram_done[a], 1)

            def axial_out(a, before, bank):
                reach(pe, widened_dve[a], before)
                reach(pe, widened_act[a], before)
                reach(pe, q1_lo[a], before)
                for s in range(G * SEQ):
                    cols = slice(s * SEQ, (s + 1) * SEQ)
                    for n, (gp, qp) in enumerate(PASSES):
                        last = pe.matmul(ps[:, bank, cols], gram_wide[a][:, gp, s].rearrange("p h e -> p (h e)"),
                                         q1[a][:, qp, cols], start=(n == 0), stop=(n == 2))
                last.then_inc(o1_done[a], 1)

            def step(i, c, load, l0, l1, ahead):
                now, before, before2, after = image(i, c), image(i, c - 1), image(i, c - 2), image(i, c + 1)
                if l0:
                    reach(pe, xn_hi[0], now)
                    reach(pe, xn_lo[0], now)
                    if c == 0:
                        pe.wait_ge(w_lo, 4)
                    reach(pe, o_scaled, before)
                    for t, m in enumerate("qk"):
                        for g in range(G):
                            last = project(ps[:, t, g * TOK:(g + 1) * TOK], w_l0[m], xn[0], g)
                    last.then_inc(qk_proj, 1)
                    reach(pe, o1_lo[0], before2)
                    for t in range(2):
                        n = 0
                        for c2 in range(2):
                            for wp, xp in PASSES:
                                last = pe.matmul(ps[:, 2, t * D:(t + 1) * D],
                                                 xn[0][:, xp, c2 * TOK + t * P:c2 * TOK + t * P + P],
                                                 w_l0["v"][:, wp, c2, :], start=(n == 0), stop=(n == 5))
                                n += 1
                    last.then_inc(v_proj, 1)
                if l1:
                    if c == 1:
                        pe.wait_ge(w_lo, 12)
                    reach(pe, xn_hi[1], before)
                    reach(pe, xn_lo[1], before)
                    reach(pe, y_copied, before2)
                    reach(pe, o1_lo[1], before2)
                    axial_proj(0, before)
                if l0:
                    reach(pe, qk_squared, now)
                    reach(pe, y_added, before2)
                    for t in range(2):
                        last = pe.matmul(ps[:, 6 + t, :], head16[:], qk_sq[:, t, :], start=True, stop=True)
                    last.then_inc(norms_done, 1)
                if l1:
                    reach(pe, kv_turned[0], before)
                    axial_proj(1, before)
                if ahead:
                    if c == -1:
                        pe.wait_ge(w_lo, 1)
                    reach(pe, v_ready, now)
                    pe.wait_ge(x_loaded[after.par], 48 * (after.half + 1))
                    for g in range(G):
                        for t in range(2):
                            last = pe.transpose(ps[:, 2, g * TOK + t * P:g * TOK + t * P + P],
                                                x_in[:, after.par, t, g * P:(g + 1) * P], ident[:])
                    last.then_inc(xt_done, 1)
                if l1:
                    if l0:
                        reach(pe, ln_done, now)
                    gram_matmuls(0, before)
                if l0:
                    reach(pe, k_masked, now)
                    for g in range(G):
                        if g == 1 and l1:
                            reach(pe, kv_turned[1], before)
                        for q in range(4):
                            bank = (0, 3)[g] + q // 2
                            for w in range(NW):
                                cols = slice(w * N, (w + 1) * N)
                                dst = ps[:, bank, (q % 2) * TOK + w * N:(q % 2) * TOK + (w + 1) * N]
                                for n, (kp, qp) in enumerate(PASSES):
                                    last = pe.matmul(dst, k_heads[:, kp, g, w, 2 * q:2 * q + 2, :].rearrange(
                                        "p h n -> p (h n)"), qk[:, qp, 0, g, cols], start=(n == 0), stop=(n == 2))
                        last.then_inc(scores_done, 1)
                if l1:
                    reach(pe, gram_summed[0], before)
                    gram_matmuls(1, before)
                    if ahead:
                        reach(pe, xt_copied, after)
                    axial_out(0, before, 2)
                if l0:
                    reach(pe, biased, now, 2)
                    reach(pe, probs_ready, now, 2)
                    for pair in range(PAIRS):
                        g, q = divmod(pair, 4)
                        last = pe.matmul(ps[32 * q:32 * q + 32, 0, g * TOK:(g + 1) * TOK], ones_pair,
                                         probs[:, pair, :], start=True, stop=True)
                    last.then_inc(den_done, 1)
                    reach(pe, v_ready, now)
                    for pair in range(PAIRS):
                        g, q = divmod(pair, 4)
                        for w in range(NW):
                            last = pe.matmul(ps[32 * q:32 * q + 32, 1, g * TOK + w * N:g * TOK + (w + 1) * N],
                                             v_diag[:, w % 2, w // 2, pair, :], probs[:, pair, w * N:(w + 1) * N],
                                             start=True, stop=True)
                    last.then_inc(pv_done, 1)
                if l1:
                    axial_out(1, before, 5)
                if ahead:
                    reach(pe, gn_small[0], after, GN_STEPS, 4)
                    if l0:
                        reach(pe, biased, now, 2)
                    pe.matmul(ps[:, 3, 0:12], group8[:], stat[0][:, 0:12], start=True, stop=True).then_inc(gn_sum[0], 1)
                if l0:
                    reach(pe, o_hi, now)
                    reach(pe, o_lo, now)
                    if l1:
                        reach(pe, gram_summed[1], before)
                    for g in range(G):
                        last = project(ps[:, 7, g * TOK:(g + 1) * TOK], w_l0["o"], o, g)
                    last.then_inc(z_proj, 1)
                if l1:
                    for a in range(2):
                        reach(pe, o1_hi[a], before)
                        reach(pe, o1_lo[a], before)
                    reach(pe, gram_summed[1], before)
                    for g in range(G):
                        n = 0
                        for a in range(2):
                            for c2 in range(2):
                                for wp, xp in PASSES:
                                    last = pe.matmul(ps[:, 6, g * TOK:(g + 1) * TOK],
                                                     w_l1[a]["o"][:, wp, c2, g * P:(g + 1) * P],
                                                     o1[a][:, xp, c2 * TOK:(c2 + 1) * TOK],
                                                     start=(n == 0), stop=(n == 11))
                                    n += 1
                    last.then_inc(y_proj, 1)
                if l0:
                    reach(pe, gn_small[1], now, GN_STEPS, 4)
                    if ahead:
                        reach(pe, gn_small[0], after, GN_STEPS, 5)
                    pe.matmul(ps[:, 3, 0:12], group8[:], stat[1][:, 0:12], start=True, stop=True).then_inc(gn_sum[1], 1)
                if l1:
                    reach(pe, y_added, before)
                    for t in range(2):
                        for g in range(G):
                            last = pe.transpose(ps[:, 4, t * D + g * P:t * D + g * P + P],
                                                y[:, g * TOK + t * P:g * TOK + t * P + P], ident[:])
                    last.then_inc(yt_done, 1)

            over_steps(pe, step)

        @block.scalar
        def _(act):
            act.preload_act_table_set("natural_log_exp_and_others")
            act.wait_ge(consts_in, 16 * N_CONST)
            act.wait_ge(hidden_done, 1)
            act.activation(table_rows[:, 0:REL * REL], ps[:, 0, 0:REL * REL], ACT.Relu,
                           bias=b1_col[:]).then_inc(hidden_relu, 1)
            act.wait_ge(table_done, 1)
            act.activation(table[:, 0, :], ps[0:HEADS, 1, 0:REL * REL], ACT.Exp, scale=-1.0).then_inc(table_exp, 1)
            act.wait_ge(table_step, 1)
            act.activation(scale_col[:, 2:3], scale_col[:, 1:2], ACT.Exp).then_inc(scale_exp, 1)
            act.wait_ge(table_step, 7)
            act.activation(q_cap[:], q_ln[:], ACT.Exp).then_inc(q_cap_exp, 1)
            for t, m in enumerate("qkvo"):
                act.wait_ge(w_turned, 1 + t)
                act.activation(w_l0[m][:, 0].rearrange("p c n -> p (c n)"), ps[:, 2 + t, :], ACT.Copy,
                               scale=WS).then_inc(w_hi, 1)
            act.wait_ge(weights_in, 16 * 8)
            for a in range(2):
                for t, m in enumerate("qkv"):
                    act.activation(w_l1[a][m][:, 0], stage_qkv[a][:, :, t * D:(t + 1) * D], ACT.Copy,
                                   scale=WS).then_inc(w_hi, 1)
                act.activation(w_l1[a]["o"][:, 0], stage_out[a], ACT.Copy, scale=WS).then_inc(w_hi, 1)

            def axial_hi(a, before):
                reach(act, kv_turned[a], before)
                reach(act, kv_widened[a], previous(before))
                act.activation(kv[a][:, :, 0, :], kv32[:], ACT.Copy).then_inc(kv_hi[a], 1)
                reach(act, q1_proj[a], before)
                reach(act, o1_done[a], previous(before))
                act.activation(in_seq(q1[a][:, 0, :]), along(ps[:, 5, :], a), ACT.Copy).then_inc(q1_hi[a], 1)

            def gram_parts(a, before):
                reach(act, gram_done[a], before)
                if a == 1:
                    reach(act, gram_summed[0], before)
                else:
                    reach(act, gram_summed[1], previous(before))
                v = ps[:, 6:8, :].rearrange("p b (s h e) -> p (b s) h e", h=2, e=DH)
                act.activation(gram_t[:].rearrange("p (s e) -> p s e", e=DH), v[:, :, 0, :], ACT.Copy,
                               scale=odd_mask_g[:, 0:1]).then_inc(gram_even[a], 1)
                reach(act, gram_summed[a], before)
                reach(act, widened_dve[a], previous(before))
                act.activation(gram[a][:, 0, :], gram32[:], ACT.Copy).then_inc(gram_hi[a], 1)

            def widen(a, before):
                reach(act, gram_lo[a], before)
                reach(act, o1_done[a], previous(before))
                src = gram[a][:].rearrange("p t (s e) -> p (t s) e", e=DH)
                dst = gram_wide[a][:].rearrange("p t s h e -> p (t s) h e")
                for h in range(ACT_HEADS):
                    last = act.activation(dst[:, :, h, :], src, ACT.Copy, scale=head_mask[:, h:h + 1])
                last.then_inc(widened_act[a], 1)

            def split_hi(layer, img):
                reach(act, gn_small[layer], img, GN_STEPS)
                prev = previous(img)
                if layer == 0:
                    reach(act, v_proj, prev)
                else:
                    reach(act, q1_proj[1], prev)
                act.activation(xn[layer][:, 0, :], xn32[layer][:], ACT.Copy).then_inc(xn_hi[layer], 1)

            def step(i, c, load, l0, l1, ahead):
                now, before, before2, after = image(i, c), image(i, c - 1), image(i, c - 2), image(i, c + 1)
                if l0:
                    reach(act, qk_proj, now)
                    reach(act, qk_scaled, before)
                    act.activation(qk_sq[:].rearrange("p t n -> p (t n)"), ps[:, 0:2, :].rearrange("p t n -> p (t n)"),
                                   ACT.Square, scale=QS / WS).then_inc(qk_squared, 1)
                if l1:
                    axial_hi(0, before)
                if l0:
                    reach(act, norms_done, now)
                    act.activation(qk_sq[:].rearrange("p t n -> p (t n)"), ps[:, 6:8, :].rearrange("p t n -> p (t n)"),
                                   ACT.Ln, bias=ln_bias).then_inc(ln_done, 1)
                    reach(act, ln_done, now)
                    for g in range(G):
                        cols = slice(g * TOK, (g + 1) * TOK)
                        act.activation(qk_sq[:, 0, cols], qk_sq[:, 0, cols], ACT.Exp, bias=q_ln[:, g:g + 1], scale=-0.5)
                    act.activation(qk_sq[:, 1, :], qk_sq[:, 1, :], ACT.Exp, bias=ln8, scale=-0.5).then_inc(rnorm_done, 1)
                    reach(act, qk_scaled, now)
                    reach(act, scores_done, before, 2)
                    act.activation(qk[:, 0].rearrange("p t g n -> p (t g n)"), qk32[:].rearrange("p t n -> p (t n)"),
                                   ACT.Copy).then_inc(qk_hi, 1)
                if l1:
                    axial_hi(1, before)
                if ahead:
                    reach(act, xt_done, after)
                    reach(act, x1_ready, before)
                    src = ps[:, 2, :].rearrange("p (a i c) -> p a i c", i=WIN, c=SIDE)
                    dst = windows(x_t[:, after.par, :])
                    act.activation(dst[:, :, 0], src[:, :, :, SHIFT:SHIFT + WIN], ACT.Copy)
                    act.activation(dst[:, :, 1, :, 0:SHIFT], src[:, :, :, SHIFT + WIN:SIDE], ACT.Copy)
                    act.activation(dst[:, :, 1, :, SHIFT:WIN], src[:, :, :, 0:SHIFT], ACT.Copy).then_inc(xt_copied, 1)
                if l1:
                    gram_parts(0, before)
                    widen(0, before)
                if l0:
                    for g in range(G):
                        reach(act, biased, now, 2, g + 1)
                        part = probs[:, 4 * g:4 * g + 4, :].rearrange("p a n -> p (a n)")
                        act.activation(part, part, ACT.Exp).then_inc(probs_ready, 1)
                if l1:
                    gram_parts(1, before)
                    widen(1, before)
                    reach(act, o1_done[0], before)
                    reach(act, y_proj, before2)
                    act.activation(along(o1[0][:, 0, :], 0), in_seq(ps[:, 2, :]), ACT.Copy).then_inc(o1_hi[0], 1)
                if l0:
                    reach(act, o_scaled, now)
                    reach(act, z_proj, before)
                    act.activation(o[:, 0, :], o32[:], ACT.Copy).then_inc(o_hi, 1)
                if l1:
                    reach(act, o1_done[1], before)
                    reach(act, y_proj, before2)
                    act.activation(along(o1[1][:, 0, :], 1), in_seq(ps[:, 5, :]), ACT.Copy).then_inc(o1_hi[1], 1)
                if ahead:
                    split_hi(0, after)
                if l0:
                    reach(act, z_proj, now)
                    reach(act, x1_ready, before)
                    for g in range(G):
                        cols = slice(g * TOK, (g + 1) * TOK)
                        last = act.activation(z[:, cols], ps[:, 7, cols], ACT.Identity, bias=bo_col[:, g:g + 1],
                                              scale=1.0 / WS)
                    last.then_inc(z_ready, 1)
                    split_hi(1, now)
                if l1:
                    reach(act, yt_done, before)
                    if not missing(image(i, c - 3).n):
                        act.wait_ge(stored[before.par], 48 * before.half)
                    act.activation(y_out[:, before.par].rearrange("p t n -> p (t n)"), ps[:, 4, :],
                                   ACT.Copy).then_inc(y_copied, 1)

            over_steps(act, step)

        @block.gpsimd
        def _(pool):
            pool.memset(v_diag[:].rearrange("p a b c d -> p (a b c d)"), 0.0).then_inc(zeroed, 1)
            pool.wait_ge(consts_in, 16 * N_CONST)

            def rstd(layer, img):
                reach(pool, gn_small[layer], img, GN_STEPS, 9)
                pool.tensor_tensor(stat[layer][:, 28:30], stat[layer][:, 26:28], minus_half,
                                   ALU.pow).then_inc(gn_pow[layer], 1)

            def split_lo(layer, img):
                reach(pool, xn_hi[layer], img)
                prev = previous(img)
                if layer == 0:
                    reach(pool, v_proj, prev)
                else:
                    reach(pool, q1_proj[1], prev)
                pool.tensor_tensor(xn[layer][:, 1, :], xn32[layer][:], xn[layer][:, 0, :],
                                   ALU.subtract).then_inc(xn_lo[layer], 1)

            def step(i, c, load, l0, l1, ahead):
                now, before, before2, after = image(i, c), image(i, c - 1), image(i, c - 2), image(i, c + 1)

                def kv_low(a):
                    reach(pool, kv_hi[a], before)
                    reach(pool, kv_widened[a], before2)
                    pool.tensor_tensor(kv[a][:, :, 1, :], kv32[:], kv[a][:, :, 0, :], ALU.subtract).then_inc(kv_lo[a], 1)

                def gram_low(a):
                    reach(pool, gram_hi[a], before)
                    pool.tensor_tensor(gram[a][:, 1, :], gram32[:], gram[a][:, 0, :], ALU.subtract).then_inc(gram_lo[a], 1)

                if l1:
                    kv_low(0)
                if l0:
                    reach(pool, qk_hi, now)
                    pool.tensor_tensor(qk[:, 1].rearrange("p t g n -> p (t g n)"),
                                       qk32[:].rearrange("p t n -> p (t n)"),
                                       qk[:, 0].rearrange("p t g n -> p (t g n)"), ALU.subtract).then_inc(qk_lo, 1)
                if l1:
                    kv_low(1)
                    gram_low(0)
                    gram_low(1)
                if ahead:
                    rstd(0, after)
                    split_lo(0, after)
                if l0:
                    rstd(1, now)
                    split_lo(1, now)

            over_steps(pool, step)

        @block.vector
        def _(dve):
            dve.wait_ge(consts_in, 16 * N_CONST)
            dve.tensor_scalar(scale_col[:, 1:2], scale_col[:, 0:1], LOG100, None, ALU.min).then_inc(table_step, 1)
            dve.wait_ge(scale_exp, 1)
            dve.tensor_scalar(scale_col[:, 3:4], scale_col[:, 2:3], SAFE_SCALE, 0.0, ALU.subtract,
                              ALU.max).then_inc(table_step, 1)
            dve.wait_ge(table_step, 2)
            dve.tensor_scalar(scale_col[:, 4:5], scale_col[:, 3:4], 8.0, None, ALU.add).then_inc(table_step, 1)
            dve.wait_ge(table_exp, 1)
            dve.tensor_scalar(table[:, 1, :], table[:, 0, :], 1.0, None, ALU.add).then_inc(table_step, 1)
            dve.wait_ge(table_step, 4)
            dve.reciprocal(table[:, 0, :], table[:, 1, :]).then_inc(table_step, 1)
            dve.wait_ge(table_step, 5)
            dve.tensor_scalar(table[:, 2, :], table[:, 0, :], 16.0, scale_col[:, 4:5], ALU.mult,
                              ALU.subtract).then_inc(table_step, 1)
            dve.tensor_scalar(q_ln[:], q_ln[:], LOG100, float(np.log(8.0)), ALU.min, ALU.add).then_inc(table_step, 1)
            dve.wait_ge(q_cap_exp, 1)
            dve.tensor_scalar(q_cap[:], q_cap[:], 1.0 / (QS * NORM_MIN), None, ALU.mult).then_inc(tables_ready, 1)
            for t, m in enumerate("qkvo"):
                dve.wait_ge(w_hi, 1 + t)
                dve.scalar_tensor_tensor(w_l0[m][:, 1].rearrange("p c n -> p (c n)"), ps[:, 2 + t, :], WS,
                                         w_l0[m][:, 0].rearrange("p c n -> p (c n)"), ALU.mult,
                                         ALU.subtract).then_inc(w_lo, 1)
            for a in range(2):
                for t, m in enumerate("qkvo"):
                    dve.wait_ge(w_hi, 5 + 4 * a + t)
                    src = stage_out[a] if m == "o" else stage_qkv[a][:, :, t * D:(t + 1) * D]
                    dve.scalar_tensor_tensor(w_l1[a][m][:, 1], src, WS, w_l1[a][m][:, 0], ALU.mult,
                                             ALU.subtract).then_inc(w_lo, 1)
            dve.wait_ge(table_in, 16 * 16)
            for w in range(NW):
                for pair in range(PAIRS):
                    seen = reach_in[:, pair, :].rearrange("p (i j) -> p i j", j=REL)[:, ::-1, WIN - 1::-1]
                    grid = "p (i j) -> p i j"
                    last = dve.tensor_tensor(bias_mask[:, pair, w, :].rearrange(grid, j=WIN), seen,
                                             mask_in[:, w, :].rearrange(grid, j=WIN), ALU.add)
            last.then_inc(tables_ready, 1)
            dve.wait_ge(tables_ready, 2)
            dve.wait_ge(zeroed, 1)

            def group_stats(layer, img, src):
                s, done = stat[layer], gn_small[layer]
                reach(dve, done, previous(img), GN_STEPS)
                for g in range(G):
                    dve.bn_stats(s[:, 6 * g:6 * g + 6], src[:, g * TOK:(g + 1) * TOK]).then_inc(done, 1)
                mean, sq_sum = s[:, 1:12:3], s[:, 2:12:3]
                reach(dve, done, img, GN_STEPS, 2)
                dve.tensor_tensor(s[:, 12:16], mean, mean, ALU.mult).then_inc(done, 1)
                reach(dve, done, img, GN_STEPS, 3)
                dve.scalar_tensor_tensor(sq_sum, sq_sum, 2.0 / TOK, s[:, 12:16], ALU.mult, ALU.add).then_inc(done, 1)

            def group_norm(layer, img, src):
                s, done = stat[layer], gn_small[layer]
                reach(dve, gn_sum[layer], img)
                dve.tensor_copy(s[:, 32:44], ps[:, 3, 0:12]).then_inc(done, 1)
                reach(dve, done, img, GN_STEPS, 5)
                half = s[:, 32:44].rearrange("p (g h v) -> p g h v", h=2, v=3)
                dve.tensor_tensor(s[:, 20:24].rearrange("p (g v) -> p g v", v=2), half[:, :, 0, 1:3],
                                  half[:, :, 1, 1:3], ALU.add).then_inc(done, 1)
                reach(dve, done, img, GN_STEPS, 6)
                dve.tensor_tensor(s[:, 24:26], s[:, 20:24:2], s[:, 20:24:2], ALU.mult).then_inc(done, 1)
                reach(dve, done, img, GN_STEPS, 7)
                dve.tensor_tensor(s[:, 30:32], s[:, 21:24:2], s[:, 24:26], ALU.subtract).then_inc(done, 1)
                reach(dve, done, img, GN_STEPS, 8)
                dve.tensor_scalar(s[:, 26:28], s[:, 30:32], 0.0, GN_EPS, ALU.max, ALU.add).then_inc(done, 1)
                reach(dve, gn_pow[layer], img)
                reach(dve, xn_lo[layer], previous(img))
                for g in range(G):
                    cols = slice(g * TOK, (g + 1) * TOK)
                    dve.tensor_scalar(xn32[layer][:, cols], src[:, cols], s[:, 20 + 2 * g:21 + 2 * g],
                                      s[:, 28 + g:29 + g], ALU.subtract, ALU.mult).then_inc(done, 1)

            def step(i, c, load, l0, l1, ahead):
                now, before, before2, after = image(i, c), image(i, c - 1), image(i, c - 2), image(i, c + 1)

                def turn(a):
                    reach(dve, kv1_proj[a], before)
                    reach(dve, kv_lo[1 - a], before if a else before2)
                    src = ps[:, 3:5, :].rearrange("p t (g r c) -> p (t g) r c", r=SIDE, c=SIDE)
                    if a == 0:
                        src = src.rearrange("p h r c -> p h c r")
                    dst = kv32[:].rearrange("p t (g s i) -> p (t g) s i", s=SEQ, i=SEQ)
                    dve.transpose(dst, src).then_inc(kv_turned[a], 1)

                def q_low(a):
                    reach(dve, q1_hi[a], before)
                    dve.tensor_tensor(in_seq(q1[a][:, 1, :]), along(ps[:, 5, :], a), in_seq(q1[a][:, 0, :]),
                                      ALU.subtract).then_inc(q1_lo[a], 1)

                def widen_kv(a):
                    reach(dve, kv_lo[a], before)
                    reach(dve, gram_done[a], before2)
                    src = kv[a][:].rearrange("p t h (s e) -> p t (h s) e", e=32)
                    k_dst = k_wide[a][:].rearrange("p t s q e -> p (t s) q e")
                    v_dst = v_wide[a][:].rearrange("p t s q e -> p (t s) q e")
                    for q in range(4):
                        dve.tensor_scalar(k_dst[:, :, q, :], src[:, 0], quad_mask[:, q:q + 1], None, ALU.mult)
                    for q in range(2):
                        last = dve.tensor_scalar(v_dst[:, :, q, :], src[:, 1], odd_mask[:, q:q + 1], None, ALU.mult)
                    last.then_inc(kv_widened[a], 1)

                def gram_sum(a):
                    reach(dve, gram_even[a], before)
                    reach(dve, gram_lo[1 - a], before if a else before2)
                    v = ps[:, 6:8, :].rearrange("p b (s h e) -> p (b s) h e", h=2, e=DH)
                    flat = "p (s e) -> p s e"
                    dve.scalar_tensor_tensor(gram32[:].rearrange(flat, e=DH), v[:, :, 1, :], odd_mask_g[:, 1:2],
                                             gram_t[:].rearrange(flat, e=DH), ALU.mult,
                                             ALU.add).then_inc(gram_summed[a], 1)

                def widen_gram(a):
                    reach(dve, gram_lo[a], before)
                    reach(dve, o1_done[a], before2)
                    src = gram[a][:].rearrange("p t (s e) -> p (t s) e", e=DH)
                    dst = gram_wide[a][:].rearrange("p t s h e -> p (t s) h e")
                    for h in range(ACT_HEADS, 8):
                        last = dve.tensor_scalar(dst[:, :, h, :], src, head_mask[:, h:h + 1], None, ALU.mult)
                    last.then_inc(widened_dve[a], 1)

                def o1_low(a, bank):
                    reach(dve, o1_hi[a], before)
                    dve.tensor_tensor(along(o1[a][:, 1, :], a), in_seq(ps[:, bank, :]), along(o1[a][:, 0, :], a),
                                      ALU.subtract).then_inc(o1_lo[a], 1)

                if l0:
                    reach(dve, v_proj, now)
                    reach(dve, pv_done, before)
                    for half in range(2):
                        rows = slice(64 * half, 64 * half + 64)
                        src = ps[rows, 2, :].rearrange("p (a b d) -> p a b d", b=2, d=DH)
                        add = bv_rows[rows].rearrange("p t (a b d) -> p (t a) b d", b=2, d=DH)
                        for b in range(2):
                            dst = v_diag[64 * b:64 * b + 64, half].rearrange("p t a d -> p (t a) d")
                            last = dve.scalar_tensor_tensor(dst[:, :, DH * b:DH * b + DH], src[:, :, b, :], 1.0 / WS,
                                                            add[:, :, b, :], ALU.mult, ALU.add)
                    last.then_inc(v_ready, 1)
                if l1:
                    turn(0)
                    q_low(0)
                    widen_kv(0)
                if l0:
                    reach(dve, rnorm_done, now)
                    reach(dve, qk_lo, before)
                    for g in range(G):
                        cols = slice(g * TOK, (g + 1) * TOK)
                        dve.scalar_tensor_tensor(qk32[:, 0, cols], qk_sq[:, 0, cols], q_cap[:, g:g + 1],
                                                 ps[:, 0, cols], ALU.min, ALU.mult)
                    dve.scalar_tensor_tensor(qk32[:, 1, :], qk_sq[:, 1, :], 8.0 / (QS * NORM_MIN),
                                             ps[:, 1, :], ALU.min, ALU.mult).then_inc(qk_scaled, 1)
                if l1:
                    turn(1)
                    q_low(1)
                if l0:
                    reach(dve, qk_lo, now)
                    reach(dve, scores_done, before, 2)
                    src = qk[:, :, 1].rearrange("p t g n -> p t (g n)").rearrange("p t (s n) -> p t s n", n=N)
                    dst = k_heads[:].rearrange("p t g w h n -> p t (g w) h n")
                    for h in range(8):
                        last = dve.tensor_scalar(dst[:, :, :, h, :], src, head_mask[:, h:h + 1], None, ALU.mult)
                    last.then_inc(k_masked, 1)
                if ahead:
                    reach(dve, xt_copied, after)
                    group_stats(0, after, x_t[:, after.par])
                if l1:
                    gram_sum(0)
                    widen_kv(1)
                if l0:
                    for g in range(G):
                        reach(dve, scores_done, now, 2, g + 1)
                        if g == 0:
                            reach(dve, pv_done, before)
                        bank = (0, 3)[g]
                        dve.tensor_tensor(probs[:, 4 * g:4 * g + 4, :].rearrange("p a n -> p (a n)"),
                                          ps[:, bank:bank + 2, :].rearrange("p b n -> p (b n)"),
                                          bias_mask[:, 4 * g:4 * g + 4].rearrange("p a w n -> p (a w n)"),
                                          ALU.add).then_inc(biased, 1)
                if l1:
                    widen_gram(0)
                    gram_sum(1)
                    widen_gram(1)
                    o1_low(0, 2)
                if l0:
                    reach(dve, den_done, now)
                    dve.reciprocal(den_inv[:], ps[:, 0, :]).then_inc(den_inverted, 1)
                    reach(dve, den_inverted, now)
                    reach(dve, pv_done, now)
                    reach(dve, o_lo, before)
                    dve.tensor_tensor(o32[:], ps[:, 1, :], den_inv[:], ALU.mult).then_inc(o_scaled, 1)
                    reach(dve, o_hi, now)
                    dve.tensor_tensor(o[:, 1, :], o32[:], o[:, 0, :], ALU.subtract).then_inc(o_lo, 1)
                if l1:
                    o1_low(1, 5)
                if ahead:
                    group_norm(0, after, x_t[:, after.par])
                if l0:
                    reach(dve, z_ready, now)
                    reach(dve, y_added, before2)
                    dst = x1[:, now.par].rearrange("p (a i b j) -> p a i b j", i=WIN, b=2, j=WIN)
                    for b in range(2):
                        last = dve.tensor_tensor(dst[:, :, :, b, :], windows(z[:])[:, :, b],
                                                 windows(x_t[:, now.par])[:, :, b], ALU.add)
                    last.then_inc(x1_ready, 1)
                    reach(dve, x1_ready, now)
                    group_stats(1, now, x1[:, now.par])
                    group_norm(1, now, x1[:, now.par])
                if l1:
                    reach(dve, y_proj, before)
                    reach(dve, yt_done, before2)
                    src, add, dst = raster(ps[:, 6, :]), raster(x1[:, before.par]), raster(y[:])
                    cut = SIDE - SHIFT
                    dve.scalar_tensor_tensor(dst[:, :, SHIFT:], src[:, :, :cut], 1.0 / (WS * WS), add[:, :, :cut],
                                             ALU.mult, ALU.add)
                    dve.scalar_tensor_tensor(dst[:, :, :SHIFT], src[:, :, cut:], 1.0 / (WS * WS), add[:, :, cut:],
                                             ALU.mult, ALU.add).then_inc(y_added, 1)

            over_steps(dve, step)


_INS = ["x", "L0_conv_Wq", "L0_conv_Wk", "L0_conv_Wv", "L0_conv_bv", "L0_conv_Wo", "L0_conv_bo",
        "L0_conv_logit_scale", "L0_conv_cpb_w1", "L0_conv_cpb_b1", "L0_conv_cpb_w2",
        "L1_conv_w_qkv0", "L1_conv_w_out0", "L1_conv_w_qkv1", "L1_conv_w_out1"]


def kernel(**inputs):
    import concourse.bacc as bacc
    from concourse.bass_utils import run_bass_kernel_spmd

    nc = bacc.Bacc("TRN2", target_bir_lowering=False, num_devices=1)
    arrays = {name: np.ascontiguousarray(inputs[name]) for name in _INS} | constants()
    args = [nc.dram_tensor(name, a.shape, mybir.dt.from_np(a.dtype), kind="ExternalInput").ap()
            for name, a in arrays.items()]
    out = nc.dram_tensor("out", (IMAGES, SIDE, SIDE, D), F32, kind="ExternalOutput").ap()
    scratch = nc.dram_tensor("position_table", (HEADS, REL * REL), F32, kind="Internal").ap()
    build(nc, *args, out, scratch)
    r = run_bass_kernel_spmd(nc, [arrays], core_ids=[0])
    return r.results[0]["out"]
```

```python
from collections import namedtuple
from contextlib import ExitStack

import numpy as np

import concourse.bass as bass
from concourse import mybir

ALU = mybir.AluOpType
ACT = mybir.ActivationFunctionType
F32 = mybir.dt.float32
F16 = mybir.dt.float16

P = 128
IMAGES, SIDE, D = 32, 16, 256
TOK = SIDE * SIDE
G = D // P
HEADS, DH = 16, 16
PAIRS = HEADS // 2
WIN, SHIFT = 8, 4
N = WIN * WIN
NW = TOK // N
SEQ = SIDE
BLOCKS = TOK // 32
REL = 2 * WIN - 1
REACH = (WIN - 1) * REL + WIN
WS = 64.0
GS = 2.0 ** -4
HALF = G * TOK
LOG100 = float(np.log(100.0))
NORM_MIN = 1e-12
QS = 8.0 * WS
LN_BIAS = 2.0 ** -63
SAFE_SCALE = 72.0
MASKED = -1.0e30
GN_EPS = 1e-5
PASSES = ((0, 0), (1, 0), (0, 1))

Image = namedtuple("Image", "n par half")


def image(i, c):
    return Image(2 * i + c, c % 2, i + c // 2)


def earlier(img, by):
    return Image(img.n - by, (img.par - by) % 2, None)


def previous(img):
    return earlier(img, 1)


def missing(n):
    return isinstance(n, int) and not 0 <= n < IMAGES


def reach(eng, sem, img, per=1, j=None):
    if not missing(img.n):
        eng.wait_ge(sem, img.n * per + (per if j is None else j))


def is_first(img):
    return isinstance(img.n, int) and img.n == 0


def edge(eng, sem, img, per=1, j=None):
    if isinstance(img.n, int):
        reach(eng, sem, img, per, j)


def constants():
    p = np.arange(P)
    ident = np.eye(P, dtype=np.float32)
    group = ((p[:, None] // 8 == p[None, :] // 8) / 16.0).astype(np.float32)
    heads = (p[:, None] // DH == p[None, :] // DH).astype(np.float32)
    halves = (p[:, None] // 64 == np.arange(32)[None, :] // DH).astype(np.float32)
    quad = (p[:, None] // 32 == np.arange(4)[None, :]).astype(np.float32)
    odd = ((p[:, None] // 16) % 2 == np.arange(2)[None, :]).astype(np.float32)
    eighth = (p[:, None] // 16 == np.arange(8)[None, :]).astype(np.float32)
    odd_g = odd * np.float32(GS / (WS * WS))
    extra = np.zeros((P, 8), np.float32)
    extra[:, 0], extra[:, 1], extra[:, 2], extra[:, 3] = LN_BIAS, np.log(8.0), -0.5, -0.5
    small = np.concatenate([halves, quad, odd, eighth, odd_g, extra], 1)
    region = np.digitize(np.arange(SIDE), [SIDE - WIN, SIDE - SHIFT])
    label = (3 * region[:, None] + region[None, :]).reshape(2, WIN, 2, WIN).transpose(0, 2, 1, 3).reshape(NW, N)
    mask = np.where(label[:, None, :] != label[:, :, None], np.float32(MASKED), np.float32(0))
    mask = np.tile(mask.transpose(2, 0, 1), (2, 1, 1)).reshape(P, NW * N).astype(np.float32)
    at = np.arange(-(WIN - 1), WIN, dtype=np.float32) / (WIN - 1) * 8.0
    at = (np.sign(at) * np.log2(np.abs(at) + 1.0) / 3.0).astype(np.float32)
    coords = np.stack(np.meshgrid(at[::-1], at[::-1], indexing="ij")).reshape(2, REL * REL).astype(np.float32)
    return {"c_ident": ident, "c_group": group, "c_heads": heads, "c_small": small, "c_mask": mask, "c_coords": coords}


def build(nc, x, Wq, Wk, Wv, bv, Wo, bo, logit_scale, cpb_w1, cpb_b1, cpb_w2, w_qkv0, w_out0, w_qkv1, w_out1,
          c_ident, c_group, c_heads, c_small, c_mask, c_coords, out, scratch):
    ctx = ExitStack()
    with ctx:
        def sb(name, shape, dt=F32):
            return ctx.enter_context(nc.sbuf_tensor(name, shape, dt))

        def sem(name):
            return ctx.enter_context(nc.semaphore(name))

        ident = sb("ident", [P, P])
        group8 = sb("group8", [P, P])
        head16 = sb("head16", [P, P])
        small = sb("small", [P, 56])
        ones_pair = small[:, 0:32]
        quad_mask = small[:, 32:36]
        odd_mask = small[:, 36:38]
        head_mask = small[:, 38:46]
        odd_mask_g = small[:, 46:48]
        ln_bias = small[:, 48:49]
        ln8 = small[:, 49:50]
        minus_half = small[:, 50:52]
        bo_col = sb("bo_col", [P, G])
        bv_rows = sb("bv_rows", [P, G, D])
        q_ln = sb("q_ln", [P, G])
        q_cap = sb("q_cap", [P, G])
        bias_mask = sb("bias_mask", [P, PAIRS, NW, N])
        w_l0 = {m: sb(f"w_{m}", [P, 2, 2, D], F16) for m in "qkvo"}
        w_l1 = [{m: sb(f"w{a}_{m}", [P, 2, 2, D], F16) for m in "qkvo"} for a in range(2)]
        x_in = sb("x_in", [P, 2, 2, D])
        x_t = sb("x_t", [P, 2, HALF])
        stat = [sb(f"stat{l}", [P, 44]) for l in range(2)]
        xn32 = [sb(f"xn32_{l}", [P, HALF]) for l in range(2)]
        xn = [sb(f"xn{l}", [P, 2, HALF], F16) for l in range(2)]
        qk_sq = sb("qk_sq", [P, 2, HALF])
        qk32 = sb("qk32", [P, 2, HALF])
        qk = sb("qk", [P, 2, 2, G, TOK], F16)
        k_heads = sb("k_heads", [P, 2, G, NW, 8, N], F16)
        v_diag = sb("v_diag", [P, 2, 2, PAIRS, 32])
        probs = sb("probs", [P, PAIRS, TOK])
        den_inv = sb("den_inv", [P, HALF])
        o32 = sb("o32", [P, HALF])
        o = sb("o", [P, 2, HALF], F16)
        z = sb("z", [P, HALF])
        x1 = sb("x1", [P, 2, HALF])
        q1 = [sb(f"q1_{a}", [P, 2, HALF], F16) for a in range(2)]
        kv32 = sb("kv32", [P, 2, HALF])
        kv = [sb(f"kv_{a}", [P, 2, 2, HALF], F16) for a in range(2)]
        k_wide = [sb(f"k_wide{a}", [P, 2, G * BLOCKS, 4, 32], F16) for a in range(2)]
        v_wide = [sb(f"v_wide{a}", [P, 2, G * BLOCKS, 2, 32], F16) for a in range(2)]
        gram_t = sb("gram_t", [P, HALF])
        gram32 = sb("gram32", [P, HALF])
        gram = [sb(f"gram{a}", [P, 2, HALF], F16) for a in range(2)]
        gram_wide = [sb(f"gram_wide{a}", [P, 2, G * SEQ, 8, 16], F16) for a in range(2)]
        o1 = [sb(f"o1_{a}", [P, 2, HALF], F16) for a in range(2)]
        y = sb("y", [P, HALF])
        y_out = sb("y_out", [P, 2, 2, D])
        ps = ctx.enter_context(nc.psum_tensor("ps", [P, 8, 512], F32))

        consts_in = sem("consts_in")
        weights_in = sem("weights_in")
        table_step = sem("table_step")
        hidden_done = sem("hidden_done")
        hidden_relu = sem("hidden_relu")
        table_done = sem("table_done")
        table_exp = sem("table_exp")
        scale_exp = sem("scale_exp")
        q_cap_exp = sem("q_cap_exp")
        tables_ready = sem("tables_ready")
        w_turned = sem("w_turned")
        w_hi = sem("w_hi")
        w_lo = sem("w_lo")
        zeroed = sem("zeroed")
        table_out = sem("table_out")
        table_in = sem("table_in")
        x_loaded = [sem(f"x_loaded{p}") for p in range(2)]
        xt_done = sem("xt_done")
        xt_copied = sem("xt_copied")
        gn_small = [sem(f"gn_small{l}") for l in range(2)]
        gn_sum = [sem(f"gn_sum{l}") for l in range(2)]
        gn_pow = [sem(f"gn_pow{l}") for l in range(2)]
        xn_hi = [sem(f"xn_hi{l}") for l in range(2)]
        xn_lo = [sem(f"xn_lo{l}") for l in range(2)]
        qk_proj = sem("qk_proj")
        v_proj = sem("v_proj")
        qk_squared = sem("qk_squared")
        norms_done = sem("norms_done")
        ln_done = sem("ln_done")
        rnorm_done = sem("rnorm_done")
        qk_scaled = sem("qk_scaled")
        qk_hi = sem("qk_hi")
        qk_lo = sem("qk_lo")
        k_masked = sem("k_masked")
        v_ready = sem("v_ready")
        scores_done = [sem(f"scores_done{g}") for g in range(G)]
        biased = [sem(f"biased{g}") for g in range(G)]
        probs_ready = [sem(f"probs_ready{g}") for g in range(G)]
        den_done = sem("den_done")
        pv_done = sem("pv_done")
        den_inverted = sem("den_inverted")
        o_scaled = sem("o_scaled")
        o_hi = sem("o_hi")
        o_lo = sem("o_lo")
        z_proj = sem("z_proj")
        z_ready = sem("z_ready")
        x1_ready = sem("x1_ready")
        kv1_proj = [sem(f"kv1_proj{a}") for a in range(2)]
        q1_proj = [sem(f"q1_proj{a}") for a in range(2)]
        kv_turned = [sem(f"kv_turned{a}") for a in range(2)]
        kv_hi = [sem(f"kv_hi{a}") for a in range(2)]
        kv_lo = [sem(f"kv_lo{a}") for a in range(2)]
        q1_hi = [sem(f"q1_hi{a}") for a in range(2)]
        q1_lo = [sem(f"q1_lo{a}") for a in range(2)]
        kv_widened = [sem(f"kv_widened{a}") for a in range(2)]
        gram_done = [sem(f"gram_done{a}") for a in range(2)]
        gram_even = [sem(f"gram_even{a}") for a in range(2)]
        gram_summed = [sem(f"gram_summed{a}") for a in range(2)]
        gram_hi = [sem(f"gram_hi{a}") for a in range(2)]
        gram_lo = [sem(f"gram_lo{a}") for a in range(2)]
        widened_dve = [sem(f"widened_dve{a}") for a in range(2)]
        widened_act = [sem(f"widened_act{a}") for a in range(2)]
        o1_done = [sem(f"o1_done{a}") for a in range(2)]
        o1_hi = [sem(f"o1_hi{a}") for a in range(2)]
        o1_lo = [sem(f"o1_lo{a}") for a in range(2)]
        y_proj = sem("y_proj")
        y_added = sem("y_added")
        yt_done = sem("yt_done")
        y_copied = sem("y_copied")
        stored = [sem(f"stored{p}") for p in range(2)]

        GN_STEPS = 11
        QK_BANK, NORM_BANK, V_BANK, DEN_BANK, PV_BANK, Z_BANK = 6, 4, 4, 3, 0, 1
        S_BANK, KV_BANK, Q_BANK = (6, 2), (2, 0), (6, 5)
        G_BANK, O_BANK, GM_BANK = (4, 0), (2, 1), (4, 7)
        Y_BANK, YT_BANK, XT_BANK = 2, 4, 2
        ACT_HEADS = 2

        stage_l0 = {"q": qk32[:, 0, :], "k": qk32[:, 1, :], "v": qk_sq[:, 0, :], "o": qk_sq[:, 1, :]}
        stage_qkv = [probs[:, 0:6, :].rearrange("p a b -> p (a b)").rearrange("p (c n) -> p c n", c=2),
                     gram_wide[0][:].rearrange("p t s h e -> p (t s h e)").bitcast(F32)[:, 0:6 * D].rearrange(
                         "p (c n) -> p c n", c=2)]
        stage_out = [kv32[:, 0, :].rearrange("p (c n) -> p c n", c=2),
                     kv32[:, 1, :].rearrange("p (c n) -> p c n", c=2)]
        mask_in = sb("mask_in", [P, NW, N])
        table_rows = z[:, :]
        reach_in = sb("reach_in", [P, PAIRS, REL * WIN])
        coords = sb("coords", [2, REL * REL])
        w1_t = sb("w1_t", [2, P])
        b1_col = sb("b1_col", [P, 1])
        w2_t = sb("w2_t", [P, HEADS])
        scale_col = sb("scale_col", [HEADS, 8])
        table = sb("table", [HEADS, 3, REL * REL])
        N_CONST = 19 + 16

        def windows(ap):
            return ap.rearrange("p (a b i j) -> p a b i j", b=2, i=WIN, j=WIN)

        def raster(ap, c=SIDE):
            return ap.rearrange("p (r c) -> p r c", c=c)

        def along(ap, a):
            v = ap.rearrange("p (g r c) -> p g r c", r=SIDE, c=SIDE)
            return v.rearrange("p g r c -> p g c r") if a == 0 else v

        def in_seq(ap):
            return ap.rearrange("p (g s i) -> p g s i", s=SEQ, i=SEQ)

        x_rows = x.rearrange("n r c d -> n (r c) d")
        out_rows = out.rearrange("n r c d -> n (r c) d")

        def pieces(rows, buf):
            s = SHIFT * SIDE
            return [(buf[:, 0, :], rows[s:s + P]), (buf[0:64, 1, :], rows[s + P:TOK]), (buf[64:P, 1, :], rows[0:s])]

        block = ctx.enter_context(nc.Block())

        STAGES = 5
        PEELED = 6
        LOOPS = (IMAGES - 2 - PEELED) // 2

        def there(i, c):
            img = image(i, c)
            return [] if missing(img.n) else [img]

        def over_steps(eng, step):
            for k in range(PEELED):
                step(0, k)
            with eng.Fori(0, LOOPS) as i:
                for u in range(2):
                    step(i, PEELED + u)
            for k in range(PEELED + 2 * LOOPS, IMAGES + STAGES - 1):
                step(0, k)

        @block.sync
        def _(sp):
            n = [0]

            def const(dst, src, **kw):
                n[0] += 1
                sp.dma_start(dst, src, **kw).then_inc(consts_in, 16)

            const(ident[:], c_ident)
            const(group8[:], c_group)
            const(head16[:], c_heads)
            const(small[:], c_small)
            const(mask_in[:].rearrange("p w n -> p (w n)"), c_mask)
            const(coords[:], c_coords)
            const(w1_t[:], cpb_w1.rearrange("h c -> c h"), allow_slow_non_contiguous=True)
            const(b1_col[:], cpb_b1.rearrange("(h a) -> h a", a=1))
            const(w2_t[:], cpb_w2.rearrange("h m -> m h"), allow_slow_non_contiguous=True)
            const(scale_col[:, 0:1], logit_scale.rearrange("h a b -> h (a b)"))
            const(bo_col[:], bo.rearrange("(g p) -> p g", p=P), allow_slow_non_contiguous=True)
            for h in range(8):
                const(q_ln[DH * h:DH * h + DH, :],
                      bass.AP(logit_scale.tensor, h, [[0, DH], [8, G], [1, 1]]), allow_slow_non_contiguous=True)
            for t in range(2):
                for rows in range(8):
                    const(bv_rows[16 * rows:16 * rows + 16, t, :], bass.AP(bv.tensor, 0, [[0, 16], [1, D]]))
            assert n[0] == N_CONST
            for m, w in (("q", Wq), ("k", Wk), ("v", Wv), ("o", Wo)):
                sp.dma_start(stage_l0[m].rearrange("p (a n) -> p a n", a=2),
                             w.rearrange("(a p) n -> p a n", p=P)).then_inc(weights_in, 16)
            for a, (wi, wo) in enumerate(((w_qkv0, w_out0), (w_qkv1, w_out1))):
                sp.dma_start(stage_qkv[a], wi.rearrange("(a p) n -> p a n", p=P)).then_inc(weights_in, 16)
                sp.dma_start(stage_out[a], wo.rearrange("(a p) n -> p a n", p=P)).then_inc(weights_in, 16)
            for b in range(2):
                for dst, src in pieces(x_rows[b], x_in[:, b]):
                    sp.dma_start(dst, src).then_inc(x_loaded[b], 16)
            sp.wait_ge(table_step, 6)
            sp.dma_start(scratch, table[:, 2, :]).then_inc(table_out, 16)
            sp.wait_ge(table_out, 16)
            for b in range(2):
                for mi in range(WIN):
                    src = bass.AP(scratch.tensor, b * REL * REL + mi * REL,
                                  [[1, WIN], [2 * REL * REL, PAIRS], [1, REACH]])
                    sp.dma_start(reach_in[64 * b + 8 * mi:64 * b + 8 * mi + 8, :, 0:REACH], src).then_inc(table_in, 16)

            def step(i, c):
                for img in there(i, c - 0):
                    for ahead in there(i, c - 0 + 2):
                        reach(sp, xt_done, img)
                        for dst, src in pieces(x_rows[ahead.n], x_in[:, ahead.par]):
                            sp.dma_start(dst, src).then_inc(x_loaded[ahead.par], 16)
                for img in there(i, c - 4):
                    reach(sp, y_copied, img)
                    for src, dst in pieces(out_rows[img.n], y_out[:, img.par]):
                        sp.dma_start(dst, src).then_inc(stored[img.par], 16)

            over_steps(sp, step)
            for b in range(2):
                sp.wait_ge(stored[b], 48 * (IMAGES // 2))

        @block.tensor
        def _(pe):
            pe.wait_ge(consts_in, 16 * N_CONST)
            pe.matmul(ps[:, 0, 0:REL * REL], w1_t[:], coords[:], start=True, stop=True).then_inc(hidden_done, 1)
            pe.wait_ge(hidden_relu, 1)
            pe.matmul(ps[0:HEADS, 1, 0:REL * REL], w2_t[:], table_rows[:, 0:REL * REL],
                      start=True, stop=True).then_inc(table_done, 1)
            pe.wait_ge(weights_in, 16 * 8)
            for t, m in enumerate("qkvo"):
                for a in range(2):
                    for c in range(2):
                        last = pe.transpose(ps[:, 2 + t, c * D + a * P:c * D + a * P + P],
                                            stage_l0[m][:, a * D + c * P:a * D + c * P + P], ident[:])
                last.then_inc(w_turned, 1)

            def project(dst, w, act, m):
                n = 0
                for c in range(2):
                    for wp, xp in PASSES:
                        last = pe.matmul(dst, w[:, wp, c, m * P:m * P + P], act[:, xp, c * TOK:(c + 1) * TOK],
                                         start=(n == 0), stop=(n == 5))
                        n += 1
                return last

            def window_qk(img):
                reach(pe, xn_hi[0], img)
                reach(pe, xn_lo[0], img)
                if is_first(img):
                    pe.wait_ge(w_lo, 4)
                reach(pe, biased[0], earlier(img, 1))
                edge(pe, q1_lo[0], earlier(img, 3))
                edge(pe, gn_small[1], earlier(img, 2), GN_STEPS, 5)
                for t, m in enumerate("qk"):
                    for g in range(G):
                        last = project(ps[:, QK_BANK + t, g * TOK:(g + 1) * TOK], w_l0[m], xn[0], g)
                last.then_inc(qk_proj, 1)

            def window_norms(img):
                reach(pe, qk_squared, img)
                reach(pe, v_ready, earlier(img, 1))
                edge(pe, gn_small[0], img, GN_STEPS, 5)
                reach(pe, q1_lo[1], earlier(img, 3))
                edge(pe, gram_summed[0], earlier(img, 3))
                for t in range(2):
                    last = pe.matmul(ps[:, NORM_BANK + t, :], head16[:], qk_sq[:, t, :], start=True, stop=True)
                last.then_inc(norms_done, 1)

            def window_v(img):
                reach(pe, xn_hi[0], img)
                reach(pe, xn_lo[0], img)
                if is_first(img):
                    pe.wait_ge(w_lo, 4)
                reach(pe, gn_small[0], earlier(img, -1), GN_STEPS, 5)
                edge(pe, y_copied, earlier(img, 3))
                for t in range(2):
                    n = 0
                    for c2 in range(2):
                        for wp, xp in PASSES:
                            last = pe.matmul(ps[:, V_BANK, t * D:(t + 1) * D],
                                             xn[0][:, xp, c2 * TOK + t * P:c2 * TOK + t * P + P],
                                             w_l0["v"][:, wp, c2, :], start=(n == 0), stop=(n == 5))
                            n += 1
                last.then_inc(v_proj, 1)

            def scores(g, img):
                reach(pe, k_masked, img)
                if g == 0:
                    reach(pe, q1_lo[0], earlier(img, 2))
                    edge(pe, qk_scaled, img)
                    reach(pe, gn_small[1], earlier(img, 1), GN_STEPS, 5)
                else:
                    reach(pe, xt_copied, earlier(img, -1))
                    edge(pe, y_added, earlier(img, 3))
                    reach(pe, den_inverted, earlier(img, 1))
                    edge(pe, kv_turned[0], earlier(img, 2))
                for q in range(4):
                    bank = S_BANK[g] + q // 2
                    for w in range(NW):
                        cols = slice(w * N, (w + 1) * N)
                        dst = ps[:, bank, (q % 2) * TOK + w * N:(q % 2) * TOK + (w + 1) * N]
                        for n, (kp, qp) in enumerate(PASSES):
                            last = pe.matmul(dst, k_heads[:, kp, g, w, 2 * q:2 * q + 2, :].rearrange(
                                "p h n -> p (h n)"), qk[:, qp, 0, g, cols], start=(n == 0), stop=(n == 2))
                last.then_inc(scores_done[g], 1)

            def window_den(img):
                for g in range(G):
                    reach(pe, probs_ready[g], img)
                reach(pe, kv_turned[0], earlier(img, 1))
                edge(pe, biased[1], img)
                for pair in range(PAIRS):
                    g, q = divmod(pair, 4)
                    last = pe.matmul(ps[32 * q:32 * q + 32, DEN_BANK, g * TOK:(g + 1) * TOK], ones_pair,
                                     probs[:, pair, :], start=True, stop=True)
                last.then_inc(den_done, 1)

            def window_pv(img):
                for g in range(G):
                    reach(pe, probs_ready[g], img)
                reach(pe, v_ready, img)
                reach(pe, kv_turned[1], earlier(img, 1))
                edge(pe, gram_summed[1], earlier(img, 2))
                for pair in range(PAIRS):
                    g, q = divmod(pair, 4)
                    for w in range(NW):
                        last = pe.matmul(ps[32 * q:32 * q + 32, PV_BANK, g * TOK + w * N:g * TOK + (w + 1) * N],
                                         v_diag[:, w % 2, w // 2, pair, :], probs[:, pair, w * N:(w + 1) * N],
                                         start=True, stop=True)
                last.then_inc(pv_done, 1)

            def window_out(img):
                reach(pe, o_hi, img)
                reach(pe, o_lo, img)
                reach(pe, o1_lo[1], earlier(img, 2))
                edge(pe, kv_turned[1], earlier(img, 1))
                edge(pe, gram_summed[1], earlier(img, 2))
                for g in range(G):
                    last = project(ps[:, Z_BANK, g * TOK:(g + 1) * TOK], w_l0["o"], o, g)
                last.then_inc(z_proj, 1)

            def axial_kv(a, img):
                reach(pe, xn_hi[1], img)
                reach(pe, xn_lo[1], img)
                if is_first(img):
                    pe.wait_ge(w_lo, 12)
                if a == 0:
                    reach(pe, biased[1], earlier(img, -1))
                    edge(pe, xt_copied, earlier(img, -2))
                    edge(pe, y_added, earlier(img, 2))
                    edge(pe, den_inverted, img)
                else:
                    reach(pe, gram_summed[1], earlier(img, 1))
                    edge(pe, o_scaled, img)
                    edge(pe, z_ready, img)
                for t, m in enumerate("kv"):
                    for g in range(G):
                        last = project(ps[:, KV_BANK[a] + t, g * TOK:(g + 1) * TOK], w_l1[a][m], xn[1], g)
                last.then_inc(kv1_proj[a], 1)

            def axial_q(a, img):
                reach(pe, xn_hi[1], img)
                reach(pe, xn_lo[1], img)
                if is_first(img):
                    pe.wait_ge(w_lo, 12)
                if a == 0:
                    reach(pe, qk_scaled, earlier(img, -2))
                    edge(pe, biased[0], earlier(img, -1))
                else:
                    reach(pe, gram_summed[0], img)
                for g in range(G):
                    last = project(ps[:, Q_BANK[a], g * TOK:(g + 1) * TOK], w_l1[a]["q"], xn[1], g)
                last.then_inc(q1_proj[a], 1)

            def gram_matmuls(a, img):
                reach(pe, kv_widened[a], img)
                if a == 0:
                    reach(pe, ln_done, earlier(img, -2))
                    edge(pe, v_ready, earlier(img, -1))
                    edge(pe, gn_small[0], earlier(img, -2), GN_STEPS, 5)
                    edge(pe, y_copied, earlier(img, 2))
                    edge(pe, q1_lo[1], earlier(img, 1))
                else:
                    reach(pe, o_scaled, earlier(img, -1))
                    edge(pe, kv_turned[1], img)
                    reach(pe, z_ready, earlier(img, -1))
                    edge(pe, o1_lo[1], earlier(img, 1))
                for s in range(G * BLOCKS):
                    dst = ps[:, G_BANK[a] + s // 8, (s % 8) * 64:(s % 8) * 64 + 64]
                    for n, (kp, vp) in enumerate(PASSES):
                        last = pe.matmul(dst, k_wide[a][:, kp, s].rearrange("p q e -> p (q e)"),
                                         v_wide[a][:, vp, s].rearrange("p q e -> p (q e)"),
                                         start=(n == 0), stop=(n == 2))
                last.then_inc(gram_done[a], 1)

            def axial_out(a, img):
                reach(pe, widened_dve[a], img)
                reach(pe, widened_act[a], img)
                reach(pe, q1_lo[a], img)
                if a == 0:
                    reach(pe, kv_turned[0], earlier(img, -1))
                    edge(pe, biased[1], earlier(img, -2))
                    edge(pe, xt_copied, earlier(img, -3))
                    edge(pe, y_added, earlier(img, 1))
                else:
                    reach(pe, kv_turned[1], earlier(img, -1))
                    edge(pe, gram_summed[1], img)
                for s in range(G * SEQ):
                    cols = slice(s * SEQ, (s + 1) * SEQ)
                    for n, (gp, qp) in enumerate(PASSES):
                        last = pe.matmul(ps[:, O_BANK[a], cols], gram_wide[a][:, gp, s].rearrange("p h e -> p (h e)"),
                                         q1[a][:, qp, cols], start=(n == 0), stop=(n == 2))
                last.then_inc(o1_done[a], 1)

            def axial_y(img):
                for a in range(2):
                    reach(pe, o1_hi[a], img)
                    reach(pe, o1_lo[a], img)
                reach(pe, o1_lo[0], img)
                for g in range(G):
                    n = 0
                    for a in range(2):
                        for c2 in range(2):
                            for wp, xp in PASSES:
                                last = pe.matmul(ps[:, Y_BANK, g * TOK:(g + 1) * TOK],
                                                 w_l1[a]["o"][:, wp, c2, g * P:(g + 1) * P],
                                                 o1[a][:, xp, c2 * TOK:(c2 + 1) * TOK],
                                                 start=(n == 0), stop=(n == 11))
                                n += 1
                last.then_inc(y_proj, 1)

            def result_rows(img):
                reach(pe, y_added, img)
                reach(pe, gram_summed[0], earlier(img, -1))
                edge(pe, ln_done, earlier(img, -3))
                edge(pe, v_ready, earlier(img, -2))
                edge(pe, gn_small[0], earlier(img, -3), GN_STEPS, 5)
                for t in range(2):
                    for g in range(G):
                        last = pe.transpose(ps[:, YT_BANK, t * D + g * P:t * D + g * P + P],
                                            y[:, g * TOK + t * P:g * TOK + t * P + P], ident[:])
                last.then_inc(yt_done, 1)

            def image_channels(img):
                pe.wait_ge(x_loaded[img.par], 48 * (img.half + 1))
                if is_first(img):
                    pe.wait_ge(w_lo, 4)
                reach(pe, y_added, earlier(img, 4))
                edge(pe, o1_lo[0], earlier(img, 4))
                edge(pe, kv_turned[0], earlier(img, 3))
                edge(pe, biased[1], earlier(img, 2))
                for g in range(G):
                    for t in range(2):
                        last = pe.transpose(ps[:, XT_BANK, g * TOK + t * P:g * TOK + t * P + P],
                                            x_in[:, img.par, t, g * P:(g + 1) * P], ident[:])
                last.then_inc(xt_done, 1)

            def group_means(layer, img):
                reach(pe, gn_small[layer], img, GN_STEPS, 4)
                if layer == 0:
                    reach(pe, y_copied, earlier(img, 4))
                    edge(pe, gram_summed[0], earlier(img, 3))
                    edge(pe, ln_done, earlier(img, 1))
                    edge(pe, v_ready, earlier(img, 2))
                else:
                    reach(pe, qk_scaled, earlier(img, -1))
                    edge(pe, biased[0], img)
                pe.matmul(ps[:, GM_BANK[layer], 0:12], group8[:], stat[layer][:, 0:12], start=True, stop=True).then_inc(
                    gn_sum[layer], 1)

            def step(i, c):
                for img in there(i, c - 0):
                    image_channels(img)
                for img in there(i, c - 4):
                    result_rows(img)
                for img in there(i, c - 2):
                    group_means(1, img)
                for img in there(i, c - 3):
                    axial_q(1, img)
                for img in there(i, c - 1):
                    scores(1, img)
                for img in there(i, c - 0):
                    group_means(0, img)
                for img in there(i, c - 1):
                    scores(0, img)
                    window_v(img)
                for img in there(i, c - 2):
                    axial_kv(0, img)
                    axial_kv(1, img)
                for img in there(i, c - 0):
                    window_qk(img)
                for img in there(i, c - 1):
                    window_den(img)
                for img in there(i, c - 3):
                    axial_out(0, img)
                for img in there(i, c - 0):
                    window_norms(img)
                for img in there(i, c - 3):
                    axial_out(1, img)
                for img in there(i, c - 1):
                    window_pv(img)
                for img in there(i, c - 2):
                    gram_matmuls(0, img)
                for img in there(i, c - 3):
                    axial_y(img)
                for img in there(i, c - 1):
                    window_out(img)
                for img in there(i, c - 2):
                    axial_q(0, img)
                    gram_matmuls(1, img)

            over_steps(pe, step)

        @block.scalar
        def _(act):
            act.preload_act_table_set("natural_log_exp_and_others")
            act.wait_ge(consts_in, 16 * N_CONST)
            act.wait_ge(hidden_done, 1)
            act.activation(table_rows[:, 0:REL * REL], ps[:, 0, 0:REL * REL], ACT.Relu,
                           bias=b1_col[:]).then_inc(hidden_relu, 1)
            act.wait_ge(table_done, 1)
            act.activation(table[:, 0, :], ps[0:HEADS, 1, 0:REL * REL], ACT.Exp, scale=-1.0).then_inc(table_exp, 1)
            act.wait_ge(table_step, 1)
            act.activation(scale_col[:, 2:3], scale_col[:, 1:2], ACT.Exp).then_inc(scale_exp, 1)
            act.wait_ge(table_step, 7)
            act.activation(q_cap[:], q_ln[:], ACT.Exp).then_inc(q_cap_exp, 1)
            for t, m in enumerate("qkvo"):
                act.wait_ge(w_turned, 1 + t)
                act.activation(w_l0[m][:, 0].rearrange("p c n -> p (c n)"), ps[:, 2 + t, :], ACT.Copy,
                               scale=WS).then_inc(w_hi, 1)
            act.wait_ge(weights_in, 16 * 8)
            for a in range(2):
                for t, m in enumerate("qkv"):
                    act.activation(w_l1[a][m][:, 0], stage_qkv[a][:, :, t * D:(t + 1) * D], ACT.Copy,
                                   scale=WS).then_inc(w_hi, 1)
                act.activation(w_l1[a]["o"][:, 0], stage_out[a], ACT.Copy, scale=WS).then_inc(w_hi, 1)

            def kv_high(a, img):
                reach(act, kv_turned[a], img)
                reach(act, kv_widened[a], previous(img))
                act.activation(kv[a][:, :, 0, :], kv32[:], ACT.Copy).then_inc(kv_hi[a], 1)

            def q1_high(a, img):
                reach(act, q1_proj[a], img)
                reach(act, o1_done[a], previous(img))
                act.activation(in_seq(q1[a][:, 0, :]), along(ps[:, Q_BANK[a], :], a), ACT.Copy).then_inc(q1_hi[a], 1)

            def gram_even_heads(a, img):
                reach(act, gram_done[a], img)
                if a == 1:
                    reach(act, gram_summed[0], img)
                else:
                    reach(act, gram_summed[1], previous(img))
                v = ps[:, G_BANK[a]:G_BANK[a] + 2, :].rearrange("p b (s h e) -> p (b s) h e", h=2, e=DH)
                act.activation(gram_t[:].rearrange("p (s e) -> p s e", e=DH), v[:, :, 0, :], ACT.Copy,
                               scale=odd_mask_g[:, 0:1]).then_inc(gram_even[a], 1)

            def gram_high(a, img):
                reach(act, gram_summed[a], img)
                reach(act, widened_dve[a], previous(img))
                reach(act, widened_act[a], previous(img))
                act.activation(gram[a][:, 0, :], gram32[:], ACT.Copy).then_inc(gram_hi[a], 1)

            def widen(a, img):
                reach(act, gram_lo[a], img)
                reach(act, o1_done[a], previous(img))
                src = gram[a][:].rearrange("p t (s e) -> p (t s) e", e=DH)
                dst = gram_wide[a][:].rearrange("p t s h e -> p (t s) h e")
                for h in range(ACT_HEADS):
                    last = act.activation(dst[:, :, h, :], src, ACT.Copy, scale=head_mask[:, h:h + 1])
                last.then_inc(widened_act[a], 1)

            def o1_high(a, img):
                reach(act, o1_done[a], img)
                reach(act, y_proj, previous(img))
                act.activation(along(o1[a][:, 0, :], a), in_seq(ps[:, O_BANK[a], :]), ACT.Copy).then_inc(o1_hi[a], 1)

            def normed_high(layer, img):
                reach(act, gn_small[layer], img, GN_STEPS)
                for read in ((qk_proj, v_proj), (*kv1_proj, *q1_proj))[layer]:
                    reach(act, read, previous(img))
                act.activation(xn[layer][:, 0, :], xn32[layer][:], ACT.Copy).then_inc(xn_hi[layer], 1)

            def probabilities(g, img):
                reach(act, biased[g], img)
                part = probs[:, 4 * g:4 * g + 4, :].rearrange("p a n -> p (a n)")
                act.activation(part, part, ACT.Exp).then_inc(probs_ready[g], 1)

            def squares(img):
                reach(act, qk_proj, img)
                reach(act, qk_scaled, previous(img))
                act.activation(qk_sq[:].rearrange("p t n -> p (t n)"), ps[:, QK_BANK:QK_BANK + 2, :].rearrange(
                    "p t n -> p (t n)"), ACT.Square, scale=QS / WS).then_inc(qk_squared, 1)

            def norm_logarithms(img):
                reach(act, norms_done, img)
                act.activation(qk_sq[:].rearrange("p t n -> p (t n)"), ps[:, NORM_BANK:NORM_BANK + 2, :].rearrange(
                    "p t n -> p (t n)"), ACT.Ln, bias=ln_bias).then_inc(ln_done, 1)

            def norm_reciprocals(img):
                reach(act, ln_done, img)
                for g in range(G):
                    cols = slice(g * TOK, (g + 1) * TOK)
                    act.activation(qk_sq[:, 0, cols], qk_sq[:, 0, cols], ACT.Exp, bias=q_ln[:, g:g + 1], scale=-0.5)
                act.activation(qk_sq[:, 1, :], qk_sq[:, 1, :], ACT.Exp, bias=ln8, scale=-0.5).then_inc(rnorm_done, 1)

            def qk_high(img):
                reach(act, qk_scaled, img)
                for g in range(G):
                    reach(act, scores_done[g], previous(img))
                reach(act, k_masked, previous(img))
                act.activation(qk[:, 0].rearrange("p t g n -> p (t g n)"), qk32[:].rearrange("p t n -> p (t n)"),
                               ACT.Copy).then_inc(qk_hi, 1)

            def o_high(img):
                reach(act, o_scaled, img)
                reach(act, z_proj, previous(img))
                act.activation(o[:, 0, :], o32[:], ACT.Copy).then_inc(o_hi, 1)

            def window_bias(img):
                reach(act, z_proj, img)
                reach(act, x1_ready, previous(img))
                for g in range(G):
                    cols = slice(g * TOK, (g + 1) * TOK)
                    last = act.activation(z[:, cols], ps[:, Z_BANK, cols], ACT.Identity, bias=bo_col[:, g:g + 1],
                                          scale=1.0 / WS)
                last.then_inc(z_ready, 1)

            def image_copy(img):
                reach(act, xt_done, img)
                reach(act, x1_ready, earlier(img, 2))
                src = ps[:, XT_BANK, :].rearrange("p (a i c) -> p a i c", i=WIN, c=SIDE)
                dst = windows(x_t[:, img.par, :])
                act.activation(dst[:, :, 0], src[:, :, :, SHIFT:SHIFT + WIN], ACT.Copy)
                act.activation(dst[:, :, 1, :, 0:SHIFT], src[:, :, :, SHIFT + WIN:SIDE], ACT.Copy)
                act.activation(dst[:, :, 1, :, SHIFT:WIN], src[:, :, :, 0:SHIFT], ACT.Copy).then_inc(xt_copied, 1)

            def result_copy(img):
                reach(act, yt_done, img)
                if not missing(earlier(img, 2).n):
                    act.wait_ge(stored[img.par], 48 * img.half)
                act.activation(y_out[:, img.par].rearrange("p t n -> p (t n)"), ps[:, YT_BANK, :],
                               ACT.Copy).then_inc(y_copied, 1)

            def step(i, c):
                for img in there(i, c - 3):
                    q1_high(0, img)
                for img in there(i, c - 0):
                    image_copy(img)
                for img in there(i, c - 3):
                    gram_even_heads(1, img)
                for img in there(i, c - 4):
                    result_copy(img)
                for img in there(i, c - 2):
                    normed_high(1, img)
                for img in there(i, c - 0):
                    normed_high(0, img)
                for img in there(i, c - 3):
                    gram_high(1, img)
                    widen(0, img)
                    q1_high(1, img)
                for img in there(i, c - 1):
                    probabilities(1, img)
                    probabilities(0, img)
                for img in there(i, c - 2):
                    kv_high(0, img)
                for img in there(i, c - 3):
                    widen(1, img)
                for img in there(i, c - 0):
                    squares(img)
                for img in there(i, c - 2):
                    kv_high(1, img)
                for img in there(i, c - 3):
                    o1_high(0, img)
                for img in there(i, c - 0):
                    norm_logarithms(img)
                for img in there(i, c - 3):
                    o1_high(1, img)
                for img in there(i, c - 0):
                    norm_reciprocals(img)
                for img in there(i, c - 1):
                    o_high(img)
                for img in there(i, c - 0):
                    qk_high(img)
                for img in there(i, c - 2):
                    gram_even_heads(0, img)
                for img in there(i, c - 1):
                    window_bias(img)
                for img in there(i, c - 2):
                    gram_high(0, img)

            over_steps(act, step)

        @block.gpsimd
        def _(pool):
            pool.memset(v_diag[:].rearrange("p a b c d -> p (a b c d)"), 0.0).then_inc(zeroed, 1)
            pool.wait_ge(consts_in, 16 * N_CONST)

            def low(dst, whole, high):
                return pool.tensor_tensor(dst, whole, high, ALU.subtract)

            def rstd(layer, img):
                reach(pool, gn_small[layer], img, GN_STEPS, 9)
                pool.tensor_tensor(stat[layer][:, 28:30], stat[layer][:, 26:28], minus_half,
                                   ALU.pow).then_inc(gn_pow[layer], 1)

            def normed_low(layer, img):
                reach(pool, xn_hi[layer], img)
                low(xn[layer][:, 1, :], xn32[layer][:], xn[layer][:, 0, :]).then_inc(xn_lo[layer], 1)

            def kv_low(a, img):
                reach(pool, kv_hi[a], img)
                low(kv[a][:, :, 1, :], kv32[:], kv[a][:, :, 0, :]).then_inc(kv_lo[a], 1)

            def gram_low(a, img):
                reach(pool, gram_hi[a], img)
                low(gram[a][:, 1, :], gram32[:], gram[a][:, 0, :]).then_inc(gram_lo[a], 1)

            def qk_low(img):
                reach(pool, qk_hi, img)
                low(qk[:, 1].rearrange("p t g n -> p (t g n)"), qk32[:].rearrange("p t n -> p (t n)"),
                    qk[:, 0].rearrange("p t g n -> p (t g n)")).then_inc(qk_lo, 1)

            def o_low(img):
                reach(pool, o_hi, img)
                low(o[:, 1, :], o32[:], o[:, 0, :]).then_inc(o_lo, 1)

            def step(i, c):
                for img in there(i, c - 4):
                    kv_low(0, img)
                    kv_low(1, img)
                for img in there(i, c - 3):
                    o_low(img)
                for img in there(i, c - 2):
                    qk_low(img)
                for img in there(i, c - 4):
                    gram_low(0, img)
                for img in there(i, c - 3):
                    rstd(1, img)
                    normed_low(1, img)
                for img in there(i, c - 1):
                    rstd(0, img)
                for img in there(i, c - 4):
                    gram_low(1, img)
                for img in there(i, c - 1):
                    normed_low(0, img)

            over_steps(pool, step)

        @block.vector
        def _(dve):
            dve.wait_ge(consts_in, 16 * N_CONST)
            dve.tensor_scalar(scale_col[:, 1:2], scale_col[:, 0:1], LOG100, None, ALU.min).then_inc(table_step, 1)
            dve.wait_ge(scale_exp, 1)
            dve.tensor_scalar(scale_col[:, 3:4], scale_col[:, 2:3], SAFE_SCALE, 0.0, ALU.subtract,
                              ALU.max).then_inc(table_step, 1)
            dve.wait_ge(table_step, 2)
            dve.tensor_scalar(scale_col[:, 4:5], scale_col[:, 3:4], 8.0, None, ALU.add).then_inc(table_step, 1)
            dve.wait_ge(table_exp, 1)
            dve.tensor_scalar(table[:, 1, :], table[:, 0, :], 1.0, None, ALU.add).then_inc(table_step, 1)
            dve.wait_ge(table_step, 4)
            dve.reciprocal(table[:, 0, :], table[:, 1, :]).then_inc(table_step, 1)
            dve.wait_ge(table_step, 5)
            dve.tensor_scalar(table[:, 2, :], table[:, 0, :], 16.0, scale_col[:, 4:5], ALU.mult,
                              ALU.subtract).then_inc(table_step, 1)
            dve.tensor_scalar(q_ln[:], q_ln[:], LOG100, float(np.log(8.0)), ALU.min, ALU.add).then_inc(table_step, 1)
            dve.wait_ge(q_cap_exp, 1)
            dve.tensor_scalar(q_cap[:], q_cap[:], 1.0 / (QS * NORM_MIN), None, ALU.mult).then_inc(tables_ready, 1)
            for t, m in enumerate("qkvo"):
                dve.wait_ge(w_hi, 1 + t)
                dve.scalar_tensor_tensor(w_l0[m][:, 1].rearrange("p c n -> p (c n)"), ps[:, 2 + t, :], WS,
                                         w_l0[m][:, 0].rearrange("p c n -> p (c n)"), ALU.mult,
                                         ALU.subtract).then_inc(w_lo, 1)
            for a in range(2):
                for t, m in enumerate("qkvo"):
                    dve.wait_ge(w_hi, 5 + 4 * a + t)
                    src = stage_out[a] if m == "o" else stage_qkv[a][:, :, t * D:(t + 1) * D]
                    dve.scalar_tensor_tensor(w_l1[a][m][:, 1], src, WS, w_l1[a][m][:, 0], ALU.mult,
                                             ALU.subtract).then_inc(w_lo, 1)
            dve.wait_ge(table_in, 16 * 16)
            for w in range(NW):
                for pair in range(PAIRS):
                    seen = reach_in[:, pair, :].rearrange("p (i j) -> p i j", j=REL)[:, ::-1, WIN - 1::-1]
                    grid = "p (i j) -> p i j"
                    last = dve.tensor_tensor(bias_mask[:, pair, w, :].rearrange(grid, j=WIN), seen,
                                             mask_in[:, w, :].rearrange(grid, j=WIN), ALU.add)
            last.then_inc(tables_ready, 1)
            dve.wait_ge(tables_ready, 2)
            dve.wait_ge(zeroed, 1)

            def group_stats(layer, img, src):
                s, done = stat[layer], gn_small[layer]
                reach(dve, done, previous(img), GN_STEPS)
                for g in range(G):
                    dve.bn_stats(s[:, 6 * g:6 * g + 6], src[:, g * TOK:(g + 1) * TOK]).then_inc(done, 1)
                mean, sq_sum = s[:, 1:12:3], s[:, 2:12:3]
                reach(dve, done, img, GN_STEPS, 2)
                dve.tensor_tensor(s[:, 12:16], mean, mean, ALU.mult).then_inc(done, 1)
                reach(dve, done, img, GN_STEPS, 3)
                dve.scalar_tensor_tensor(sq_sum, sq_sum, 2.0 / TOK, s[:, 12:16], ALU.mult, ALU.add).then_inc(done, 1)

            def group_var(layer, img):
                s, done = stat[layer], gn_small[layer]
                reach(dve, gn_sum[layer], img)
                dve.tensor_copy(s[:, 32:44], ps[:, GM_BANK[layer], 0:12]).then_inc(done, 1)
                reach(dve, done, img, GN_STEPS, 5)
                half = s[:, 32:44].rearrange("p (g h v) -> p g h v", h=2, v=3)
                dve.tensor_tensor(s[:, 20:24].rearrange("p (g v) -> p g v", v=2), half[:, :, 0, 1:3],
                                  half[:, :, 1, 1:3], ALU.add).then_inc(done, 1)
                reach(dve, done, img, GN_STEPS, 6)
                dve.tensor_tensor(s[:, 24:26], s[:, 20:24:2], s[:, 20:24:2], ALU.mult).then_inc(done, 1)
                reach(dve, done, img, GN_STEPS, 7)
                dve.tensor_tensor(s[:, 30:32], s[:, 21:24:2], s[:, 24:26], ALU.subtract).then_inc(done, 1)
                reach(dve, done, img, GN_STEPS, 8)
                dve.tensor_scalar(s[:, 26:28], s[:, 30:32], 0.0, GN_EPS, ALU.max, ALU.add).then_inc(done, 1)

            def group_norm(layer, img, src):
                s, done = stat[layer], gn_small[layer]
                reach(dve, gn_pow[layer], img)
                reach(dve, xn_lo[layer], previous(img))
                for g in range(G):
                    cols = slice(g * TOK, (g + 1) * TOK)
                    dve.tensor_scalar(xn32[layer][:, cols], src[:, cols], s[:, 20 + 2 * g:21 + 2 * g],
                                      s[:, 28 + g:29 + g], ALU.subtract, ALU.mult).then_inc(done, 1)

            def turn(a, img):
                reach(dve, kv1_proj[a], img)
                reach(dve, kv_lo[1 - a], img if a else previous(img))
                src = ps[:, KV_BANK[a]:KV_BANK[a] + 2, :].rearrange("p t (g r c) -> p (t g) r c", r=SIDE, c=SIDE)
                if a == 0:
                    src = src.rearrange("p h r c -> p h c r")
                dst = kv32[:].rearrange("p t (g s i) -> p (t g) s i", s=SEQ, i=SEQ)
                dve.transpose(dst, src).then_inc(kv_turned[a], 1)

            def q1_low(a, img):
                reach(dve, q1_hi[a], img)
                dve.tensor_tensor(in_seq(q1[a][:, 1, :]), along(ps[:, Q_BANK[a], :], a), in_seq(q1[a][:, 0, :]),
                                  ALU.subtract).then_inc(q1_lo[a], 1)

            def widen_kv(a, img):
                reach(dve, kv_lo[a], img)
                reach(dve, gram_done[a], previous(img))
                src = kv[a][:].rearrange("p t h (s e) -> p t (h s) e", e=32)
                k_dst = k_wide[a][:].rearrange("p t s q e -> p (t s) q e")
                v_dst = v_wide[a][:].rearrange("p t s q e -> p (t s) q e")
                for q in range(4):
                    dve.tensor_scalar(k_dst[:, :, q, :], src[:, 0], quad_mask[:, q:q + 1], None, ALU.mult)
                for q in range(2):
                    last = dve.tensor_scalar(v_dst[:, :, q, :], src[:, 1], odd_mask[:, q:q + 1], None, ALU.mult)
                last.then_inc(kv_widened[a], 1)

            def gram_sum(a, img):
                reach(dve, gram_even[a], img)
                reach(dve, gram_lo[1 - a], img if a else previous(img))
                v = ps[:, G_BANK[a]:G_BANK[a] + 2, :].rearrange("p b (s h e) -> p (b s) h e", h=2, e=DH)
                flat = "p (s e) -> p s e"
                dve.scalar_tensor_tensor(gram32[:].rearrange(flat, e=DH), v[:, :, 1, :], odd_mask_g[:, 1:2],
                                         gram_t[:].rearrange(flat, e=DH), ALU.mult,
                                         ALU.add).then_inc(gram_summed[a], 1)

            def widen_gram(a, img):
                reach(dve, gram_lo[a], img)
                reach(dve, o1_done[a], previous(img))
                src = gram[a][:].rearrange("p t (s e) -> p (t s) e", e=DH)
                dst = gram_wide[a][:].rearrange("p t s h e -> p (t s) h e")
                for h in range(ACT_HEADS, 8):
                    last = dve.tensor_scalar(dst[:, :, h, :], src, head_mask[:, h:h + 1], None, ALU.mult)
                last.then_inc(widened_dve[a], 1)

            def o1_low(a, img):
                reach(dve, o1_hi[a], img)
                dve.tensor_tensor(along(o1[a][:, 1, :], a), in_seq(ps[:, O_BANK[a], :]), along(o1[a][:, 0, :], a),
                                  ALU.subtract).then_inc(o1_lo[a], 1)

            def spread_v(img):
                reach(dve, v_proj, img)
                reach(dve, pv_done, previous(img))
                for half in range(2):
                    rows = slice(64 * half, 64 * half + 64)
                    src = ps[rows, V_BANK, :].rearrange("p (a b d) -> p a b d", b=2, d=DH)
                    add = bv_rows[rows].rearrange("p t (a b d) -> p (t a) b d", b=2, d=DH)
                    for b in range(2):
                        dst = v_diag[64 * b:64 * b + 64, half].rearrange("p t a d -> p (t a) d")
                        last = dve.scalar_tensor_tensor(dst[:, :, DH * b:DH * b + DH], src[:, :, b, :], 1.0 / WS,
                                                        add[:, :, b, :], ALU.mult, ALU.add)
                last.then_inc(v_ready, 1)

            def scale_qk(img):
                reach(dve, rnorm_done, img)
                reach(dve, qk_lo, previous(img))
                for g in range(G):
                    cols = slice(g * TOK, (g + 1) * TOK)
                    dve.scalar_tensor_tensor(qk32[:, 0, cols], qk_sq[:, 0, cols], q_cap[:, g:g + 1],
                                             ps[:, QK_BANK, cols], ALU.min, ALU.mult)
                dve.scalar_tensor_tensor(qk32[:, 1, :], qk_sq[:, 1, :], 8.0 / (QS * NORM_MIN),
                                         ps[:, QK_BANK + 1, :], ALU.min, ALU.mult).then_inc(qk_scaled, 1)

            def mask_k(img):
                reach(dve, qk_lo, img)
                for g in range(G):
                    reach(dve, scores_done[g], previous(img))
                src = qk[:, :, 1].rearrange("p t g n -> p t (g n)").rearrange("p t (s n) -> p t s n", n=N)
                dst = k_heads[:].rearrange("p t g w h n -> p t (g w) h n")
                for h in range(8):
                    last = dve.tensor_scalar(dst[:, :, :, h, :], src, head_mask[:, h:h + 1], None, ALU.mult)
                last.then_inc(k_masked, 1)

            def add_bias(g, img):
                reach(dve, scores_done[g], img)
                reach(dve, den_done, previous(img))
                reach(dve, pv_done, previous(img))
                dve.tensor_tensor(probs[:, 4 * g:4 * g + 4, :].rearrange("p a n -> p (a n)"),
                                  ps[:, S_BANK[g]:S_BANK[g] + 2, :].rearrange("p b n -> p (b n)"),
                                  bias_mask[:, 4 * g:4 * g + 4].rearrange("p a w n -> p (a w n)"),
                                  ALU.add).then_inc(biased[g], 1)

            def invert_den(img):
                reach(dve, den_done, img)
                reach(dve, o_scaled, previous(img))
                dve.reciprocal(den_inv[:], ps[:, DEN_BANK, :]).then_inc(den_inverted, 1)

            def scale_o(img):
                reach(dve, den_inverted, img)
                reach(dve, pv_done, img)
                reach(dve, o_lo, previous(img))
                dve.tensor_tensor(o32[:], ps[:, PV_BANK, :], den_inv[:], ALU.mult).then_inc(o_scaled, 1)

            def add_x(img):
                reach(dve, z_ready, img)
                reach(dve, y_added, earlier(img, 2))
                dst = x1[:, img.par].rearrange("p (a i b j) -> p a i b j", i=WIN, b=2, j=WIN)
                for b in range(2):
                    last = dve.tensor_tensor(dst[:, :, :, b, :], windows(z[:])[:, :, b],
                                             windows(x_t[:, img.par])[:, :, b], ALU.add)
                last.then_inc(x1_ready, 1)

            def group_stats0(img):
                reach(dve, xt_copied, img)
                group_stats(0, img, x_t[:, img.par])

            def group_stats1(img):
                reach(dve, x1_ready, img)
                group_stats(1, img, x1[:, img.par])

            def add_x1(img):
                reach(dve, y_proj, img)
                reach(dve, yt_done, previous(img))
                src, add, dst = raster(ps[:, Y_BANK, :]), raster(x1[:, img.par]), raster(y[:])
                edge = SIDE - SHIFT
                dve.scalar_tensor_tensor(dst[:, :, SHIFT:], src[:, :, :edge], 1.0 / (WS * WS), add[:, :, :edge],
                                         ALU.mult, ALU.add)
                dve.scalar_tensor_tensor(dst[:, :, :SHIFT], src[:, :, edge:], 1.0 / (WS * WS), add[:, :, edge:],
                                         ALU.mult, ALU.add).then_inc(y_added, 1)

            def step(i, c):
                for img in there(i, c - 3):
                    turn(0, img)
                for img in there(i, c - 2):
                    spread_v(img)
                for img in there(i, c - 4):
                    widen_gram(1, img)
                    q1_low(1, img)
                for img in there(i, c - 3):
                    turn(1, img)
                    widen_kv(0, img)
                for img in there(i, c - 2):
                    invert_den(img)
                for img in there(i, c - 4):
                    o1_low(0, img)
                    o1_low(1, img)
                for img in there(i, c - 2):
                    scale_o(img)
                for img in there(i, c - 1):
                    scale_qk(img)
                for img in there(i, c - 3):
                    widen_kv(1, img)
                    gram_sum(0, img)
                for img in there(i, c - 1):
                    mask_k(img)
                for img in there(i, c - 4):
                    add_x1(img)
                for img in there(i, c - 2):
                    add_x(img)
                    group_stats1(img)
                for img in there(i, c - 3):
                    q1_low(0, img)
                for img in there(i, c - 2):
                    group_var(1, img)
                for img in there(i, c - 0):
                    group_stats0(img)
                for img in there(i, c - 2):
                    group_norm(1, img, x1[:, img.par])
                for img in there(i, c - 0):
                    group_var(0, img)
                for img in there(i, c - 1):
                    add_bias(1, img)
                for img in there(i, c - 0):
                    group_norm(0, img, x_t[:, img.par])
                for img in there(i, c - 3):
                    gram_sum(1, img)
                    widen_gram(0, img)
                for img in there(i, c - 1):
                    add_bias(0, img)

            over_steps(dve, step)


_INS = ["x", "L0_conv_Wq", "L0_conv_Wk", "L0_conv_Wv", "L0_conv_bv", "L0_conv_Wo", "L0_conv_bo",
        "L0_conv_logit_scale", "L0_conv_cpb_w1", "L0_conv_cpb_b1", "L0_conv_cpb_w2",
        "L1_conv_w_qkv0", "L1_conv_w_out0", "L1_conv_w_qkv1", "L1_conv_w_out1"]


def kernel(**inputs):
    import concourse.bacc as bacc
    from concourse.bass_utils import run_bass_kernel_spmd

    nc = bacc.Bacc("TRN2", target_bir_lowering=False, num_devices=1)
    arrays = {name: np.ascontiguousarray(inputs[name]) for name in _INS} | constants()
    args = [nc.dram_tensor(name, a.shape, mybir.dt.from_np(a.dtype), kind="ExternalInput").ap()
            for name, a in arrays.items()]
    out = nc.dram_tensor("out", (IMAGES, SIDE, SIDE, D), F32, kind="ExternalOutput").ap()
    scratch = nc.dram_tensor("position_table", (HEADS, REL * REL), F32, kind="Internal").ap()
    build(nc, *args, out, scratch)
    r = run_bass_kernel_spmd(nc, [arrays], core_ids=[0])
    return r.results[0]["out"]
```

```python
from collections import namedtuple
from contextlib import ExitStack

import numpy as np

import concourse.bass as bass
from concourse import mybir

ALU = mybir.AluOpType
ACT = mybir.ActivationFunctionType
F32 = mybir.dt.float32
F16 = mybir.dt.float16

P = 128
IMAGES, SIDE, D = 32, 16, 256
TOK = SIDE * SIDE
G = D // P
HEADS, DH = 16, 16
PAIRS = HEADS // 2
WIN, SHIFT = 8, 4
N = WIN * WIN
NW = TOK // N
SEQ = SIDE
BLOCKS = TOK // 32
REL = 2 * WIN - 1
REACH = (WIN - 1) * REL + WIN
WS = 64.0
GS = 2.0 ** -4
HALF = G * TOK
UNROLL = 4
LOG100 = float(np.log(100.0))
NORM_MIN = 1e-12
QS = 8.0 * WS
LN_BIAS = 2.0 ** -63
SAFE_SCALE = 72.0
MASKED = -1.0e30
GN_EPS = 1e-5
PASSES = ((0, 0), (1, 0), (0, 1))

Image = namedtuple("Image", "n par half")


def image(i, c):
    return Image(UNROLL * i + c, c % 2, UNROLL // 2 * i + c // 2)


def earlier(img, by):
    return Image(img.n - by, (img.par - by) % 2, None)


def previous(img):
    return earlier(img, 1)


def missing(n):
    return isinstance(n, int) and not 0 <= n < IMAGES


def reach(eng, sem, img, per=1, j=None):
    if not missing(img.n):
        eng.wait_ge(sem, img.n * per + (per if j is None else j))


def is_first(img):
    return isinstance(img.n, int) and img.n == 0


def edge(eng, sem, img, per=1, j=None):
    if isinstance(img.n, int):
        reach(eng, sem, img, per, j)


def constants():
    p = np.arange(P)
    ident = np.eye(P, dtype=np.float32)
    group = ((p[:, None] // 8 == p[None, :] // 8) / 16.0).astype(np.float32)
    heads = (p[:, None] // DH == p[None, :] // DH).astype(np.float32)
    halves = (p[:, None] // 64 == np.arange(32)[None, :] // DH).astype(np.float32)
    quad = (p[:, None] // 32 == np.arange(4)[None, :]).astype(np.float32)
    odd = ((p[:, None] // 16) % 2 == np.arange(2)[None, :]).astype(np.float32)
    eighth = (p[:, None] // 16 == np.arange(8)[None, :]).astype(np.float32)
    odd_g = odd * np.float32(GS / (WS * WS))
    extra = np.zeros((P, 8), np.float32)
    extra[:, 0], extra[:, 1], extra[:, 2], extra[:, 3] = LN_BIAS, np.log(8.0), -0.5, -0.5
    small = np.concatenate([halves, quad, odd, eighth, odd_g, extra], 1)
    region = np.digitize(np.arange(SIDE), [SIDE - WIN, SIDE - SHIFT])
    label = (3 * region[:, None] + region[None, :]).reshape(2, WIN, 2, WIN).transpose(0, 2, 1, 3).reshape(NW, N)
    mask = np.where(label[:, None, :] != label[:, :, None], np.float32(MASKED), np.float32(0))
    mask = np.tile(mask.transpose(2, 0, 1), (2, 1, 1)).reshape(P, NW * N).astype(np.float32)
    at = np.arange(-(WIN - 1), WIN, dtype=np.float32) / (WIN - 1) * 8.0
    at = (np.sign(at) * np.log2(np.abs(at) + 1.0) / 3.0).astype(np.float32)
    coords = np.stack(np.meshgrid(at[::-1], at[::-1], indexing="ij")).reshape(2, REL * REL).astype(np.float32)
    return {"c_ident": ident, "c_group": group, "c_heads": heads, "c_small": small, "c_mask": mask, "c_coords": coords}


def build(nc, x, Wq, Wk, Wv, bv, Wo, bo, logit_scale, cpb_w1, cpb_b1, cpb_w2, w_qkv0, w_out0, w_qkv1, w_out1,
          c_ident, c_group, c_heads, c_small, c_mask, c_coords, out, scratch):
    ctx = ExitStack()
    with ctx:
        def sb(name, shape, dt=F32):
            return ctx.enter_context(nc.sbuf_tensor(name, shape, dt))

        def sem(name):
            return ctx.enter_context(nc.semaphore(name))

        ident = sb("ident", [P, P])
        group8 = sb("group8", [P, P])
        head16 = sb("head16", [P, P])
        small = sb("small", [P, 56])
        ones_pair = small[:, 0:32]
        quad_mask = small[:, 32:36]
        odd_mask = small[:, 36:38]
        head_mask = small[:, 38:46]
        odd_mask_g = small[:, 46:48]
        ln_bias = small[:, 48:49]
        ln8 = small[:, 49:50]
        minus_half = small[:, 50:52]
        bo_col = sb("bo_col", [P, G])
        bv_rows = sb("bv_rows", [P, G, D])
        q_ln = sb("q_ln", [P, G])
        q_cap = sb("q_cap", [P, G])
        bias_mask = sb("bias_mask", [P, PAIRS, NW, N])
        w_l0 = {m: sb(f"w_{m}", [P, 2, 2, D], F16) for m in "qkvo"}
        w_l1 = [{m: sb(f"w{a}_{m}", [P, 2, 2, D], F16) for m in "qkvo"} for a in range(2)]
        x_in = sb("x_in", [P, 2, 2, D])
        x_t = sb("x_t", [P, 2, HALF])
        stat = [sb(f"stat{l}", [P, 32]) for l in range(2)]
        xn32 = [sb(f"xn32_{l}", [P, HALF]) for l in range(2)]
        xn = [sb(f"xn{l}", [P, 2, HALF], F16) for l in range(2)]
        qk_sq = sb("qk_sq", [P, 2, HALF])
        qk32 = sb("qk32", [P, 2, HALF])
        qk = sb("qk", [P, 2, 2, G, TOK], F16)
        k_heads = sb("k_heads", [P, 2, G, NW, 8, N], F16)
        v_diag = sb("v_diag", [P, 2, 2, PAIRS, 32])
        probs = sb("probs", [P, PAIRS, TOK])
        den_inv = sb("den_inv", [P, HALF])
        o32 = sb("o32", [P, HALF])
        o = sb("o", [P, 2, HALF], F16)
        z = sb("z", [P, HALF])
        x1 = sb("x1", [P, 2, HALF])
        q1_32 = [sb(f"q1_32_{a}", [P, HALF]) for a in range(2)]
        q1 = [sb(f"q1_{a}", [P, 2, HALF], F16) for a in range(2)]
        kv32 = sb("kv32", [P, 2, HALF])
        kv = [sb(f"kv_{a}", [P, 2, 2, HALF], F16) for a in range(2)]
        k_wide = [sb(f"k_wide{a}", [P, 2, G * BLOCKS, 4, 32], F16) for a in range(2)]
        v_wide = [sb(f"v_wide{a}", [P, 2, G * BLOCKS, 2, 32], F16) for a in range(2)]
        gram_t = sb("gram_t", [P, HALF])
        gram32 = sb("gram32", [P, HALF])
        gram = [sb(f"gram{a}", [P, 2, HALF], F16) for a in range(2)]
        gram_wide = [sb(f"gram_wide{a}", [P, 2, G * SEQ, 8, 16], F16) for a in range(2)]
        o1_32 = [sb(f"o1_32_{a}", [P, HALF]) for a in range(2)]
        o1 = [sb(f"o1_{a}", [P, 2, HALF], F16) for a in range(2)]
        y = sb("y", [P, HALF])
        y_out = sb("y_out", [P, 2, 2, D])
        ps = ctx.enter_context(nc.psum_tensor("ps", [P, 8, 512], F32))

        first_in = sem("first_in")
        table_in = sem("table_in")
        w0_in = sem("w0_in")
        scale_in = sem("scale_in")
        late_in = sem("late_in")
        w1_in = sem("w1_in")
        table_step = sem("table_step")
        hidden_done = sem("hidden_done")
        hidden_relu = sem("hidden_relu")
        table_done = sem("table_done")
        table_exp = sem("table_exp")
        scale_exp = sem("scale_exp")
        q_cap_exp = sem("q_cap_exp")
        tables_ready = sem("tables_ready")
        bias_ready = sem("bias_ready")
        w_turned = sem("w_turned")
        w_hi = sem("w_hi")
        w_lo = sem("w_lo")
        zeroed = sem("zeroed")
        table_out = sem("table_out")
        rows_in = sem("rows_in")
        x_loaded = [sem(f"x_loaded{p}") for p in range(2)]
        xt_done = sem("xt_done")
        xt_copied = sem("xt_copied")
        gn_small = [sem(f"gn_small{l}") for l in range(2)]
        gn_sum = [sem(f"gn_sum{l}") for l in range(2)]
        gn_pow = [sem(f"gn_pow{l}") for l in range(2)]
        xn_hi = [sem(f"xn_hi{l}") for l in range(2)]
        xn_lo = [sem(f"xn_lo{l}") for l in range(2)]
        qk_proj = sem("qk_proj")
        v_proj = sem("v_proj")
        qk_squared = sem("qk_squared")
        norms_done = sem("norms_done")
        ln_done = sem("ln_done")
        rnorm_done = sem("rnorm_done")
        qk_scaled = sem("qk_scaled")
        qk_hi = sem("qk_hi")
        qk_lo = sem("qk_lo")
        k_masked = sem("k_masked")
        v_ready = sem("v_ready")
        scores_done = [sem(f"scores_done{g}") for g in range(G)]
        biased = [sem(f"biased{g}") for g in range(G)]
        probs_ready = [sem(f"probs_ready{g}") for g in range(G)]
        den_done = sem("den_done")
        pv_done = sem("pv_done")
        den_inverted = sem("den_inverted")
        o_scaled = sem("o_scaled")
        o_hi = sem("o_hi")
        o_lo = sem("o_lo")
        z_proj = sem("z_proj")
        z_ready = sem("z_ready")
        x1_ready = sem("x1_ready")
        kv1_proj = [sem(f"kv1_proj{a}") for a in range(2)]
        q1_proj = [sem(f"q1_proj{a}") for a in range(2)]
        kv_turned = [sem(f"kv_turned{a}") for a in range(2)]
        kv_hi = [sem(f"kv_hi{a}") for a in range(2)]
        kv_lo = [sem(f"kv_lo{a}") for a in range(2)]
        q1_copied = [sem(f"q1_copied{a}") for a in range(2)]
        q1_hi = [sem(f"q1_hi{a}") for a in range(2)]
        q1_lo = [sem(f"q1_lo{a}") for a in range(2)]
        kv_widened = [sem(f"kv_widened{a}") for a in range(2)]
        gram_done = [sem(f"gram_done{a}") for a in range(2)]
        gram_even = [sem(f"gram_even{a}") for a in range(2)]
        gram_summed = [sem(f"gram_summed{a}") for a in range(2)]
        gram_hi = [sem(f"gram_hi{a}") for a in range(2)]
        gram_lo = [sem(f"gram_lo{a}") for a in range(2)]
        widened_dve = [sem(f"widened_dve{a}") for a in range(2)]
        widened_act = [sem(f"widened_act{a}") for a in range(2)]
        o1_done = [sem(f"o1_done{a}") for a in range(2)]
        o1_aside = [sem(f"o1_aside{a}") for a in range(2)]
        o1_summed = [sem(f"o1_summed{a}") for a in range(2)]
        o1_hi = [sem(f"o1_hi{a}") for a in range(2)]
        o1_lo = [sem(f"o1_lo{a}") for a in range(2)]
        y_proj = sem("y_proj")
        y_added = sem("y_added")
        yt_done = sem("yt_done")
        y_copied = sem("y_copied")
        stored = [sem(f"stored{p}") for p in range(2)]

        GN_STEPS = 10
        QK_BANK, NORM_BANK, V_BANK, DEN_BANK, PV_BANK, Z_BANK = 6, 4, 4, 2, 3, 4
        S_BANK, KV_BANK, Q_BANK = (0, 0), (2, 4), (3, 5)
        G_BANK, O_BANK, GM_BANK = (0, 6), (6, 0), (5, 3)
        Y_BANK, YT_BANK, XT_BANK = 5, 3, 2
        ACT_HEADS = 3

        stage_l0 = {"q": qk32[:, 0, :], "k": qk32[:, 1, :], "v": qk_sq[:, 0, :], "o": qk_sq[:, 1, :]}
        stage_qkv = [probs[:, 0:6, :].rearrange("p a b -> p (a b)").rearrange("p (c n) -> p c n", c=2),
                     gram_wide[0][:].rearrange("p t s h e -> p (t s h e)").bitcast(F32)[:, 0:6 * D].rearrange(
                         "p (c n) -> p c n", c=2)]
        stage_out = [kv32[:, 0, :].rearrange("p (c n) -> p c n", c=2),
                     kv32[:, 1, :].rearrange("p (c n) -> p c n", c=2)]
        idle = gram_wide[1][:].rearrange("p t s h e -> p (t s h e)").bitcast(F32)
        reach_in = idle[:, 0:PAIRS * REL * WIN].rearrange("p (a n) -> p a n", a=PAIRS)
        mask_in = idle[:, PAIRS * REL * WIN:PAIRS * REL * WIN + NW * N].rearrange("p (w n) -> p w n", n=N)
        table_rows = z[:, :]
        coords = sb("coords", [2, REL * REL])
        w1_t = sb("w1_t", [2, P])
        b1_col = sb("b1_col", [P, 1])
        w2_t = sb("w2_t", [P, HEADS])
        scale_col = sb("scale_col", [HEADS, 8])
        table = sb("table", [HEADS, 3, REL * REL])

        def windows(ap):
            return ap.rearrange("p (a b i j) -> p a b i j", b=2, i=WIN, j=WIN)

        def raster(ap, c=SIDE):
            return ap.rearrange("p (r c) -> p r c", c=c)

        def along(ap, a):
            v = ap.rearrange("p (g r c) -> p g r c", r=SIDE, c=SIDE)
            return v.rearrange("p g r c -> p g c r") if a == 0 else v

        def in_seq(ap):
            return ap.rearrange("p (g s i) -> p g s i", s=SEQ, i=SEQ)

        x_rows = x.rearrange("n r c d -> n (r c) d")
        out_rows = out.rearrange("n r c d -> n (r c) d")

        def pieces(rows, buf):
            s = SHIFT * SIDE
            return [(buf[:, 0, :], rows[s:s + P]), (buf[0:64, 1, :], rows[s + P:TOK]), (buf[64:P, 1, :], rows[0:s])]

        block = ctx.enter_context(nc.Block())

        STAGES = 5
        PEELED = 6
        LOOPS = (IMAGES - 2 - PEELED) // UNROLL

        def there(i, c):
            img = image(i, c)
            return [] if missing(img.n) else [img]

        def over_steps(eng, step):
            for k in range(PEELED):
                step(0, k)
            with eng.Fori(0, LOOPS) as i:
                for u in range(UNROLL):
                    step(i, PEELED + u)
            for k in range(PEELED + UNROLL * LOOPS, IMAGES + STAGES - 1):
                step(0, k)

        @block.sync
        def _(sp):
            def load(dst, src, arrived, **kw):
                sp.dma_start(dst, src, **kw).then_inc(arrived, 16)

            def load_image(n):
                for dst, src in pieces(x_rows[n], x_in[:, n]):
                    load(dst, src, x_loaded[n])

            load(ident[:], c_ident, first_in)
            load(small[:], c_small, first_in)
            load(group8[:], c_group, first_in)
            load(coords[:], c_coords, table_in)
            load(w1_t[:], cpb_w1.rearrange("h c -> c h"), table_in, allow_slow_non_contiguous=True)
            load(b1_col[:], cpb_b1.rearrange("(h a) -> h a", a=1), table_in)
            load(w2_t[:], cpb_w2.rearrange("h m -> m h"), table_in, allow_slow_non_contiguous=True)
            load(scale_col[:, 0:1], logit_scale.rearrange("h a b -> h (a b)"), table_in)
            load_image(0)
            for m, w in (("q", Wq), ("k", Wk), ("v", Wv), ("o", Wo)):
                load(stage_l0[m].rearrange("p (a n) -> p a n", a=2), w.rearrange("(a p) n -> p a n", p=P), w0_in)
            for h in range(8):
                load(q_ln[DH * h:DH * h + DH, :], bass.AP(logit_scale.tensor, h, [[0, DH], [8, G], [1, 1]]), scale_in,
                     allow_slow_non_contiguous=True)
            load(head16[:], c_heads, late_in)
            load(mask_in, c_mask.rearrange("p (w n) -> p w n", n=N), late_in)
            load(bo_col[:], bo.rearrange("(g p) -> p g", p=P), late_in, allow_slow_non_contiguous=True)
            for t in range(2):
                load(bv_rows[:, t, :], bass.AP(bv.tensor, 0, [[0, P], [1, D]]), late_in)
            for a, (wi, wo) in enumerate(((w_qkv0, w_out0), (w_qkv1, w_out1))):
                load(stage_qkv[a], wi.rearrange("(a p) n -> p a n", p=P), w1_in)
                load(stage_out[a], wo.rearrange("(a p) n -> p a n", p=P), w1_in)
            load_image(1)
            sp.wait_ge(table_step, 6)
            sp.dma_start(scratch, table[:, 2, :]).then_inc(table_out, 16)
            sp.wait_ge(table_out, 16)
            for b in range(2):
                for mi in range(WIN):
                    src = bass.AP(scratch.tensor, b * REL * REL + mi * REL,
                                  [[1, WIN], [2 * REL * REL, PAIRS], [1, REACH]])
                    sp.dma_start(reach_in[64 * b + 8 * mi:64 * b + 8 * mi + 8, :, 0:REACH], src).then_inc(rows_in, 16)

            def step(i, c):
                for img in there(i, c):
                    for ahead in there(i, c - 0 + 2):
                        reach(sp, xt_done, img)
                        for dst, src in pieces(x_rows[ahead.n], x_in[:, ahead.par]):
                            sp.dma_start(dst, src).then_inc(x_loaded[ahead.par], 16)
                for img in there(i, c - 4):
                    reach(sp, y_copied, img)
                    for src, dst in pieces(out_rows[img.n], y_out[:, img.par]):
                        sp.dma_start(dst, src).then_inc(stored[img.par], 16)

            over_steps(sp, step)
            for b in range(2):
                sp.wait_ge(stored[b], 48 * (IMAGES // 2))

        @block.tensor
        def _(pe):
            pe.wait_ge(first_in, 16 * 3)
            pe.wait_ge(table_in, 16 * 5)
            pe.matmul(ps[:, 0, 0:REL * REL], w1_t[:], coords[:], start=True, stop=True).then_inc(hidden_done, 1)
            pe.wait_ge(hidden_relu, 1)
            pe.matmul(ps[0:HEADS, 1, 0:REL * REL], w2_t[:], table_rows[:, 0:REL * REL],
                      start=True, stop=True).then_inc(table_done, 1)
            pe.wait_ge(w0_in, 16 * 4)
            for t, m in enumerate("qkvo"):
                for a in range(2):
                    for c in range(2):
                        last = pe.transpose(ps[:, 2 + t, c * D + a * P:c * D + a * P + P],
                                            stage_l0[m][:, a * D + c * P:a * D + c * P + P], ident[:])
                last.then_inc(w_turned, 1)

            def project(dst, w, act, m):
                n = 0
                for c in range(2):
                    for wp, xp in PASSES:
                        last = pe.matmul(dst, w[:, wp, c, m * P:m * P + P], act[:, xp, c * TOK:(c + 1) * TOK],
                                         start=(n == 0), stop=(n == 5))
                        n += 1
                return last

            def window_qk(img):
                reach(pe, xn_hi[0], img)
                reach(pe, xn_lo[0], img)
                if is_first(img):
                    pe.wait_ge(w_lo, 4)
                reach(pe, o1_summed[0], earlier(img, 3))
                edge(pe, gram_summed[1], earlier(img, 3))
                for t, m in enumerate("qk"):
                    for g in range(G):
                        last = project(ps[:, QK_BANK + t, g * TOK:(g + 1) * TOK], w_l0[m], xn[0], g)
                last.then_inc(qk_proj, 1)

            def window_norms(img):
                if is_first(img):
                    pe.wait_ge(late_in, 16 * 5)
                reach(pe, qk_squared, img)
                reach(pe, kv_turned[1], earlier(img, 2))
                edge(pe, v_ready, earlier(img, 1))
                edge(pe, z_ready, earlier(img, 2))
                edge(pe, gn_small[0], img, GN_STEPS, 5)
                for t in range(2):
                    last = pe.matmul(ps[:, NORM_BANK + t, :], head16[:], qk_sq[:, t, :], start=True, stop=True)
                last.then_inc(norms_done, 1)

            def window_v(img):
                reach(pe, xn_hi[0], img)
                reach(pe, xn_lo[0], img)
                if is_first(img):
                    pe.wait_ge(w_lo, 4)
                reach(pe, z_ready, earlier(img, 1))
                edge(pe, ln_done, img)
                for t in range(2):
                    n = 0
                    for c2 in range(2):
                        for wp, xp in PASSES:
                            last = pe.matmul(ps[:, V_BANK, t * D:(t + 1) * D],
                                             xn[0][:, xp, c2 * TOK + t * P:c2 * TOK + t * P + P],
                                             w_l0["v"][:, wp, c2, :], start=(n == 0), stop=(n == 5))
                            n += 1
                last.then_inc(v_proj, 1)

            def scores(g, img):
                reach(pe, k_masked, img)
                if g == 0:
                    reach(pe, biased[1], img)
                else:
                    reach(pe, gram_summed[0], earlier(img, 2))
                    edge(pe, o1_summed[1], earlier(img, 3))
                    edge(pe, biased[0], earlier(img, 1))
                for q in range(4):
                    bank = S_BANK[g] + q // 2
                    for w in range(NW):
                        cols = slice(w * N, (w + 1) * N)
                        dst = ps[:, bank, (q % 2) * TOK + w * N:(q % 2) * TOK + (w + 1) * N]
                        for n, (kp, qp) in enumerate(PASSES):
                            last = pe.matmul(dst, k_heads[:, kp, g, w, 2 * q:2 * q + 2, :].rearrange(
                                "p h n -> p (h n)"), qk[:, qp, 0, g, cols], start=(n == 0), stop=(n == 2))
                last.then_inc(scores_done[g], 1)

            def window_den(img):
                for g in range(G):
                    reach(pe, probs_ready[g], img)
                reach(pe, kv_turned[0], earlier(img, 1))
                edge(pe, xt_copied, earlier(img, -1))
                for pair in range(PAIRS):
                    g, q = divmod(pair, 4)
                    last = pe.matmul(ps[32 * q:32 * q + 32, DEN_BANK, g * TOK:(g + 1) * TOK], ones_pair,
                                     probs[:, pair, :], start=True, stop=True)
                last.then_inc(den_done, 1)

            def window_pv(img):
                for g in range(G):
                    reach(pe, probs_ready[g], img)
                reach(pe, v_ready, img)
                reach(pe, kv_turned[0], earlier(img, 1))
                edge(pe, y_copied, earlier(img, 3))
                edge(pe, gn_small[1], earlier(img, 1), GN_STEPS, 5)
                edge(pe, q1_copied[0], earlier(img, 2))
                for pair in range(PAIRS):
                    g, q = divmod(pair, 4)
                    for w in range(NW):
                        last = pe.matmul(ps[32 * q:32 * q + 32, PV_BANK, g * TOK + w * N:g * TOK + (w + 1) * N],
                                         v_diag[:, w % 2, w // 2, pair, :], probs[:, pair, w * N:(w + 1) * N],
                                         start=True, stop=True)
                last.then_inc(pv_done, 1)

            def window_out(img):
                reach(pe, o_hi, img)
                reach(pe, o_lo, img)
                reach(pe, ln_done, earlier(img, -1))
                edge(pe, kv_turned[1], earlier(img, 1))
                for g in range(G):
                    last = project(ps[:, Z_BANK, g * TOK:(g + 1) * TOK], w_l0["o"], o, g)
                last.then_inc(z_proj, 1)

            def axial_kv(a, img):
                reach(pe, xn_hi[1], img)
                reach(pe, xn_lo[1], img)
                if is_first(img):
                    pe.wait_ge(w_lo, 12)
                if a == 0:
                    reach(pe, xt_copied, earlier(img, -2))
                    edge(pe, den_inverted, img)
                    reach(pe, y_copied, earlier(img, 2))
                    edge(pe, gn_small[1], img, GN_STEPS, 5)
                else:
                    reach(pe, v_ready, earlier(img, -1))
                    edge(pe, z_ready, img)
                    reach(pe, gn_small[0], earlier(img, -2), GN_STEPS, 5)
                    edge(pe, q1_copied[1], earlier(img, 1))
                for t, m in enumerate("kv"):
                    for g in range(G):
                        last = project(ps[:, KV_BANK[a] + t, g * TOK:(g + 1) * TOK], w_l1[a][m], xn[1], g)
                last.then_inc(kv1_proj[a], 1)

            def axial_q(a, img):
                reach(pe, xn_hi[1], img)
                reach(pe, xn_lo[1], img)
                if is_first(img):
                    pe.wait_ge(w_lo, 12)
                if a == 0:
                    reach(pe, o_scaled, earlier(img, -1))
                    edge(pe, kv_turned[0], img)
                else:
                    reach(pe, y_added, earlier(img, 1))
                    edge(pe, ln_done, earlier(img, -2))
                for g in range(G):
                    last = project(ps[:, Q_BANK[a], g * TOK:(g + 1) * TOK], w_l1[a]["q"], xn[1], g)
                last.then_inc(q1_proj[a], 1)

            def gram_matmuls(a, img):
                reach(pe, kv_widened[a], img)
                if a == 0:
                    reach(pe, o1_summed[1], earlier(img, 1))
                    edge(pe, biased[0], earlier(img, -1))
                else:
                    reach(pe, qk_scaled, earlier(img, -2))
                    edge(pe, o1_summed[0], earlier(img, 1))
                for s in range(G * BLOCKS):
                    dst = ps[:, G_BANK[a] + s // 8, (s % 8) * 64:(s % 8) * 64 + 64]
                    for n, (kp, vp) in enumerate(PASSES):
                        last = pe.matmul(dst, k_wide[a][:, kp, s].rearrange("p q e -> p (q e)"),
                                         v_wide[a][:, vp, s].rearrange("p q e -> p (q e)"),
                                         start=(n == 0), stop=(n == 2))
                last.then_inc(gram_done[a], 1)

            def axial_out(a, img):
                reach(pe, widened_dve[a], img)
                reach(pe, widened_act[a], img)
                reach(pe, q1_lo[a], img)
                if a == 0:
                    reach(pe, gram_summed[1], img)
                else:
                    reach(pe, biased[0], earlier(img, -2))
                    edge(pe, biased[1], earlier(img, -2))
                    edge(pe, gram_summed[0], img)
                for s in range(G * SEQ):
                    cols = slice(s * SEQ, (s + 1) * SEQ)
                    dst = ps[:, O_BANK[a] + s // SEQ, (s % SEQ) * 2 * SEQ:(s % SEQ + 1) * 2 * SEQ]
                    high, low = (gram_wide[a][:, gp, s].rearrange("p h e -> p (h e)") for gp in range(2))
                    pe.matmul(dst.rearrange("p (t i) -> p t i", t=2), high, q1[a][:, :, cols], start=True, stop=False)
                    last = pe.matmul(dst[:, 0:SEQ], low, q1[a][:, 0, cols], start=False, stop=True)
                last.then_inc(o1_done[a], 1)

            def axial_y(img):
                for a in range(2):
                    reach(pe, o1_hi[a], img)
                    reach(pe, o1_lo[a], img)
                reach(pe, ln_done, earlier(img, -3))
                edge(pe, kv_turned[1], earlier(img, -1))
                edge(pe, gn_small[0], earlier(img, -3), GN_STEPS, 5)
                edge(pe, q1_copied[1], img)
                for g in range(G):
                    n = 0
                    for a in range(2):
                        for c2 in range(2):
                            for wp, xp in PASSES:
                                last = pe.matmul(ps[:, Y_BANK, g * TOK:(g + 1) * TOK],
                                                 w_l1[a]["o"][:, wp, c2, g * P:(g + 1) * P],
                                                 o1[a][:, xp, c2 * TOK:(c2 + 1) * TOK],
                                                 start=(n == 0), stop=(n == 11))
                                n += 1
                last.then_inc(y_proj, 1)

            def result_rows(img):
                reach(pe, y_added, img)
                reach(pe, gn_small[1], earlier(img, -2), GN_STEPS, 5)
                edge(pe, q1_copied[0], earlier(img, -1))
                edge(pe, o_scaled, earlier(img, -2))
                edge(pe, kv_turned[0], earlier(img, -1))
                for t in range(2):
                    for g in range(G):
                        last = pe.transpose(ps[:, YT_BANK, t * D + g * P:t * D + g * P + P],
                                            y[:, g * TOK + t * P:g * TOK + t * P + P], ident[:])
                last.then_inc(yt_done, 1)

            def image_channels(img):
                pe.wait_ge(x_loaded[img.par], 48 * (img.half + 1))
                if is_first(img):
                    pe.wait_ge(w_lo, 4)
                reach(pe, den_inverted, earlier(img, 2))
                edge(pe, kv_turned[0], earlier(img, 3))
                for g in range(G):
                    for t in range(2):
                        last = pe.transpose(ps[:, XT_BANK, g * TOK + t * P:g * TOK + t * P + P],
                                            x_in[:, img.par, t, g * P:(g + 1) * P], ident[:])
                last.then_inc(xt_done, 1)

            def group_means(layer, img):
                reach(pe, gn_small[layer], img, GN_STEPS, 4)
                if layer == 0:
                    reach(pe, q1_copied[1], earlier(img, 3))
                    edge(pe, y_added, earlier(img, 4))
                    edge(pe, ln_done, earlier(img, 1))
                    edge(pe, kv_turned[1], earlier(img, 3))
                else:
                    reach(pe, q1_copied[0], earlier(img, 1))
                    edge(pe, o_scaled, img)
                halves = stat[layer][:, 0:12].rearrange("p (g h v) -> p g h v", h=2, v=3)
                for h in range(2):
                    last = pe.matmul(ps[:, GM_BANK[layer], 0:6].rearrange("p (g v) -> p g v", v=3), group8[:],
                                     halves[:, :, h, :], start=(h == 0), stop=(h == 1))
                last.then_inc(gn_sum[layer], 1)

            def step(i, c):
                for img in there(i, c - 2):
                    window_pv(img)
                for img in there(i, c - 4):
                    axial_y(img)
                for img in there(i, c - 3):
                    axial_q(0, img)
                for img in there(i, c - 2):
                    window_out(img)
                for img in there(i, c - 3):
                    gram_matmuls(1, img)
                for img in there(i, c):
                    image_channels(img)
                for img in there(i, c - 3):
                    axial_q(1, img)
                for img in there(i, c - 1):
                    scores(1, img)
                for img in there(i, c - 2):
                    group_means(1, img)
                for img in there(i, c - 1):
                    window_v(img)
                for img in there(i, c - 4):
                    result_rows(img)
                for img in there(i, c - 3):
                    axial_out(0, img)
                for img in there(i, c - 1):
                    scores(0, img)
                for img in there(i, c):
                    group_means(0, img)
                for img in there(i, c - 2):
                    axial_kv(0, img)
                    axial_kv(1, img)
                for img in there(i, c):
                    window_qk(img)
                for img in there(i, c - 3):
                    axial_out(1, img)
                for img in there(i, c - 1):
                    window_den(img)
                for img in there(i, c):
                    window_norms(img)
                for img in there(i, c - 2):
                    gram_matmuls(0, img)

            over_steps(pe, step)

        @block.scalar
        def _(act):
            act.preload_act_table_set("natural_log_exp_and_others")
            act.wait_ge(first_in, 16 * 3)
            act.wait_ge(table_in, 16 * 5)
            act.wait_ge(hidden_done, 1)
            act.activation(table_rows[:, 0:REL * REL], ps[:, 0, 0:REL * REL], ACT.Relu,
                           bias=b1_col[:]).then_inc(hidden_relu, 1)
            act.wait_ge(table_done, 1)
            act.activation(table[:, 0, :], ps[0:HEADS, 1, 0:REL * REL], ACT.Exp, scale=-1.0).then_inc(table_exp, 1)
            act.wait_ge(table_step, 1)
            act.activation(scale_col[:, 2:3], scale_col[:, 1:2], ACT.Exp).then_inc(scale_exp, 1)
            act.wait_ge(table_step, 7)
            act.activation(q_cap[:], q_ln[:], ACT.Exp).then_inc(q_cap_exp, 1)
            for t, m in enumerate("qkvo"):
                act.wait_ge(w_turned, 1 + t)
                act.activation(w_l0[m][:, 0].rearrange("p c n -> p (c n)"), ps[:, 2 + t, :], ACT.Copy,
                               scale=WS).then_inc(w_hi, 1)

            def axial_weights_high():
                act.wait_ge(w1_in, 16 * 4)
                for a in range(2):
                    for t, m in enumerate("qkv"):
                        act.activation(w_l1[a][m][:, 0], stage_qkv[a][:, :, t * D:(t + 1) * D], ACT.Copy,
                                       scale=WS).then_inc(w_hi, 1)
                    act.activation(w_l1[a]["o"][:, 0], stage_out[a], ACT.Copy, scale=WS).then_inc(w_hi, 1)

            def kv_high(a, img):
                reach(act, kv_turned[a], img)
                reach(act, kv_widened[a], previous(img))
                act.activation(kv[a][:, :, 0, :], kv32[:], ACT.Copy).then_inc(kv_hi[a], 1)

            def q1_copy(a, img):
                reach(act, q1_proj[a], img)
                reach(act, q1_lo[a], previous(img))
                act.activation(in_seq(q1_32[a][:]), along(ps[:, Q_BANK[a], :], a), ACT.Copy).then_inc(q1_copied[a], 1)

            def q1_high(a, img):
                reach(act, q1_copied[a], img)
                reach(act, o1_done[a], previous(img))
                act.activation(q1[a][:, 0, :], q1_32[a][:], ACT.Copy).then_inc(q1_hi[a], 1)

            def gram_even_heads(a, img):
                reach(act, gram_done[a], img)
                if a == 1:
                    reach(act, gram_summed[0], img)
                else:
                    reach(act, gram_summed[1], previous(img))
                v = ps[:, G_BANK[a]:G_BANK[a] + 2, :].rearrange("p b (s h e) -> p (b s) h e", h=2, e=DH)
                act.activation(gram_t[:].rearrange("p (s e) -> p s e", e=DH), v[:, :, 0, :], ACT.Copy,
                               scale=odd_mask_g[:, 0:1]).then_inc(gram_even[a], 1)

            def gram_high(a, img):
                reach(act, gram_summed[a], img)
                reach(act, widened_dve[a], previous(img))
                reach(act, widened_act[a], previous(img))
                act.activation(gram[a][:, 0, :], gram32[:], ACT.Copy).then_inc(gram_hi[a], 1)

            def widen(a, img):
                reach(act, gram_lo[a], img)
                reach(act, o1_done[a], previous(img))
                src = gram[a][:].rearrange("p t (s e) -> p (t s) e", e=DH)
                dst = gram_wide[a][:].rearrange("p t s h e -> p (t s) h e")
                for h in range(ACT_HEADS):
                    last = act.activation(dst[:, :, h, :], src, ACT.Copy, scale=head_mask[:, h:h + 1])
                last.then_inc(widened_act[a], 1)

            def o1_side(a, img):
                reach(act, o1_done[a], img)
                reach(act, o1_lo[a], previous(img))
                both = ps[:, O_BANK[a]:O_BANK[a] + 2, :].rearrange("p b (s t i) -> p (b s) t i", t=2, i=SEQ)
                act.activation(o1_32[a][:].rearrange("p (s i) -> p s i", i=SEQ), both[:, :, 1, :],
                               ACT.Copy).then_inc(o1_aside[a], 1)

            def o1_high(a, img):
                reach(act, o1_summed[a], img)
                reach(act, y_proj, previous(img))
                act.activation(along(o1[a][:, 0, :], a), in_seq(o1_32[a][:]), ACT.Copy).then_inc(o1_hi[a], 1)

            def normed_high(layer, img):
                reach(act, gn_small[layer], img, GN_STEPS)
                for read in ((qk_proj, v_proj), (*kv1_proj, *q1_proj))[layer]:
                    reach(act, read, previous(img))
                act.activation(xn[layer][:, 0, :], xn32[layer][:], ACT.Copy).then_inc(xn_hi[layer], 1)

            def probabilities(g, img):
                reach(act, biased[g], img)
                part = probs[:, 4 * g:4 * g + 4, :].rearrange("p a n -> p (a n)")
                act.activation(part, part, ACT.Exp).then_inc(probs_ready[g], 1)

            def squares(img):
                if is_first(img):
                    axial_weights_high()
                reach(act, qk_proj, img)
                reach(act, qk_scaled, previous(img))
                act.activation(qk_sq[:].rearrange("p t n -> p (t n)"), ps[:, QK_BANK:QK_BANK + 2, :].rearrange(
                    "p t n -> p (t n)"), ACT.Square, scale=QS / WS).then_inc(qk_squared, 1)

            def norm_logarithms(img):
                reach(act, norms_done, img)
                act.activation(qk_sq[:].rearrange("p t n -> p (t n)"), ps[:, NORM_BANK:NORM_BANK + 2, :].rearrange(
                    "p t n -> p (t n)"), ACT.Ln, bias=ln_bias).then_inc(ln_done, 1)

            def norm_reciprocals(img):
                reach(act, ln_done, img)
                for g in range(G):
                    cols = slice(g * TOK, (g + 1) * TOK)
                    act.activation(qk_sq[:, 0, cols], qk_sq[:, 0, cols], ACT.Exp, bias=q_ln[:, g:g + 1], scale=-0.5)
                act.activation(qk_sq[:, 1, :], qk_sq[:, 1, :], ACT.Exp, bias=ln8, scale=-0.5).then_inc(rnorm_done, 1)

            def qk_high(img):
                reach(act, qk_scaled, img)
                for g in range(G):
                    reach(act, scores_done[g], previous(img))
                reach(act, k_masked, previous(img))
                act.activation(qk[:, 0].rearrange("p t g n -> p (t g n)"), qk32[:].rearrange("p t n -> p (t n)"),
                               ACT.Copy).then_inc(qk_hi, 1)

            def o_high(img):
                reach(act, o_scaled, img)
                reach(act, z_proj, previous(img))
                act.activation(o[:, 0, :], o32[:], ACT.Copy).then_inc(o_hi, 1)

            def window_bias(img):
                if is_first(img):
                    act.wait_ge(late_in, 16 * 5)
                reach(act, z_proj, img)
                reach(act, x1_ready, previous(img))
                for g in range(G):
                    cols = slice(g * TOK, (g + 1) * TOK)
                    last = act.activation(z[:, cols], ps[:, Z_BANK, cols], ACT.Identity, bias=bo_col[:, g:g + 1],
                                          scale=1.0 / WS)
                last.then_inc(z_ready, 1)

            def image_copy(img):
                reach(act, xt_done, img)
                reach(act, x1_ready, earlier(img, 2))
                src = ps[:, XT_BANK, :].rearrange("p (a i c) -> p a i c", i=WIN, c=SIDE)
                dst = windows(x_t[:, img.par, :])
                act.activation(dst[:, :, 0], src[:, :, :, SHIFT:SHIFT + WIN], ACT.Copy)
                act.activation(dst[:, :, 1, :, 0:SHIFT], src[:, :, :, SHIFT + WIN:SIDE], ACT.Copy)
                act.activation(dst[:, :, 1, :, SHIFT:WIN], src[:, :, :, 0:SHIFT], ACT.Copy).then_inc(xt_copied, 1)

            def result_copy(img):
                reach(act, yt_done, img)
                if not missing(earlier(img, 2).n):
                    act.wait_ge(stored[img.par], 48 * img.half)
                act.activation(y_out[:, img.par].rearrange("p t n -> p (t n)"), ps[:, YT_BANK, :],
                               ACT.Copy).then_inc(y_copied, 1)

            def step(i, c):
                for img in there(i, c - 3):
                    gram_high(0, img)
                for img in there(i, c - 2):
                    o_high(img)
                for img in there(i, c - 1):
                    qk_high(img)
                for img in there(i, c - 3):
                    widen(0, img)
                    q1_copy(0, img)
                for img in there(i, c - 2):
                    window_bias(img)
                for img in there(i, c - 3):
                    q1_high(0, img)
                    gram_even_heads(1, img)
                    q1_copy(1, img)
                    gram_high(1, img)
                    q1_high(1, img)
                for img in there(i, c):
                    image_copy(img)
                for img in there(i, c - 4):
                    result_copy(img)
                for img in there(i, c - 2):
                    normed_high(1, img)
                for img in there(i, c - 3):
                    o1_side(0, img)
                    widen(1, img)
                for img in there(i, c):
                    normed_high(0, img)
                for img in there(i, c - 2):
                    kv_high(0, img)
                for img in there(i, c - 1):
                    probabilities(0, img)
                for img in there(i, c - 3):
                    o1_high(0, img)
                for img in there(i, c - 1):
                    probabilities(1, img)
                for img in there(i, c):
                    squares(img)
                for img in there(i, c - 2):
                    kv_high(1, img)
                for img in there(i, c - 3):
                    o1_side(1, img)
                    o1_high(1, img)
                for img in there(i, c):
                    norm_logarithms(img)
                for img in there(i, c - 2):
                    gram_even_heads(0, img)
                for img in there(i, c):
                    norm_reciprocals(img)

            over_steps(act, step)

        @block.gpsimd
        def _(pool):
            pool.memset(v_diag[:].rearrange("p a b c d -> p (a b c d)"), 0.0).then_inc(zeroed, 1)
            pool.wait_ge(first_in, 16 * 3)

            def low(dst, whole, high):
                return pool.tensor_tensor(dst, whole, high, ALU.subtract)

            def rstd(layer, img):
                reach(pool, gn_small[layer], img, GN_STEPS, 8)
                pool.tensor_tensor(stat[layer][:, 28:30], stat[layer][:, 26:28], minus_half,
                                   ALU.pow).then_inc(gn_pow[layer], 1)

            def normed_low(layer, img):
                reach(pool, xn_hi[layer], img)
                low(xn[layer][:, 1, :], xn32[layer][:], xn[layer][:, 0, :]).then_inc(xn_lo[layer], 1)

            def kv_low(a, img):
                reach(pool, kv_hi[a], img)
                low(kv[a][:, :, 1, :], kv32[:], kv[a][:, :, 0, :]).then_inc(kv_lo[a], 1)

            def gram_low(a, img):
                reach(pool, gram_hi[a], img)
                low(gram[a][:, 1, :], gram32[:], gram[a][:, 0, :]).then_inc(gram_lo[a], 1)

            def qk_low(img):
                reach(pool, qk_hi, img)
                low(qk[:, 1].rearrange("p t g n -> p (t g n)"), qk32[:].rearrange("p t n -> p (t n)"),
                    qk[:, 0].rearrange("p t g n -> p (t g n)")).then_inc(qk_lo, 1)

            def q1_low(a, img):
                reach(pool, q1_hi[a], img)
                low(q1[a][:, 1, :], q1_32[a][:], q1[a][:, 0, :]).then_inc(q1_lo[a], 1)

            def o1_low(a, img):
                reach(pool, o1_hi[a], img)
                low(along(o1[a][:, 1, :], a), in_seq(o1_32[a][:]), along(o1[a][:, 0, :], a)).then_inc(o1_lo[a], 1)

            def o_low(img):
                reach(pool, o_hi, img)
                low(o[:, 1, :], o32[:], o[:, 0, :]).then_inc(o_lo, 1)

            def step(i, c):
                for img in there(i, c - 4):
                    gram_low(1, img)
                for img in there(i, c - 3):
                    normed_low(1, img)
                for img in there(i, c - 4):
                    q1_low(1, img)
                for img in there(i, c - 1):
                    rstd(0, img)
                    normed_low(0, img)
                for img in there(i, c - 3):
                    kv_low(0, img)
                    kv_low(1, img)
                for img in there(i, c - 4):
                    o1_low(0, img)
                    o1_low(1, img)
                for img in there(i, c - 3):
                    gram_low(0, img)
                for img in there(i, c - 2):
                    o_low(img)
                for img in there(i, c - 1):
                    qk_low(img)
                for img in there(i, c - 3):
                    q1_low(0, img)
                for img in there(i, c - 2):
                    rstd(1, img)

            over_steps(pool, step)

        @block.vector
        def _(dve):
            dve.wait_ge(first_in, 16 * 3)
            dve.wait_ge(table_in, 16 * 5)
            dve.tensor_scalar(scale_col[:, 1:2], scale_col[:, 0:1], LOG100, None, ALU.min).then_inc(table_step, 1)
            dve.wait_ge(scale_exp, 1)
            dve.tensor_scalar(scale_col[:, 3:4], scale_col[:, 2:3], SAFE_SCALE, 0.0, ALU.subtract,
                              ALU.max).then_inc(table_step, 1)
            dve.wait_ge(table_step, 2)
            dve.tensor_scalar(scale_col[:, 4:5], scale_col[:, 3:4], 8.0, None, ALU.add).then_inc(table_step, 1)
            dve.wait_ge(table_exp, 1)
            dve.tensor_scalar(table[:, 1, :], table[:, 0, :], 1.0, None, ALU.add).then_inc(table_step, 1)
            dve.wait_ge(table_step, 4)
            dve.reciprocal(table[:, 0, :], table[:, 1, :]).then_inc(table_step, 1)
            dve.wait_ge(table_step, 5)
            dve.tensor_scalar(table[:, 2, :], table[:, 0, :], 16.0, scale_col[:, 4:5], ALU.mult,
                              ALU.subtract).then_inc(table_step, 1)
            dve.wait_ge(scale_in, 16 * 8)
            dve.tensor_scalar(q_ln[:], q_ln[:], LOG100, float(np.log(8.0)), ALU.min, ALU.add).then_inc(table_step, 1)
            dve.wait_ge(q_cap_exp, 1)
            dve.tensor_scalar(q_cap[:], q_cap[:], 1.0 / (QS * NORM_MIN), None, ALU.mult).then_inc(tables_ready, 1)
            for t, m in enumerate("qkvo"):
                dve.wait_ge(w_hi, 1 + t)
                dve.scalar_tensor_tensor(w_l0[m][:, 1].rearrange("p c n -> p (c n)"), ps[:, 2 + t, :], WS,
                                         w_l0[m][:, 0].rearrange("p c n -> p (c n)"), ALU.mult,
                                         ALU.subtract).then_inc(w_lo, 1)
            dve.wait_ge(zeroed, 1)

            def axial_weights_low():
                for a in range(2):
                    for t, m in enumerate("qkvo"):
                        dve.wait_ge(w_hi, 5 + 4 * a + t)
                        src = stage_out[a] if m == "o" else stage_qkv[a][:, :, t * D:(t + 1) * D]
                        dve.scalar_tensor_tensor(w_l1[a][m][:, 1], src, WS, w_l1[a][m][:, 0], ALU.mult,
                                                 ALU.subtract).then_inc(w_lo, 1)

            def bias_tables():
                dve.wait_ge(rows_in, 16 * 16)
                dve.wait_ge(late_in, 16 * 5)
                for w in range(NW):
                    for pair in range(PAIRS):
                        seen = reach_in[:, pair, :].rearrange("p (i j) -> p i j", j=REL)[:, ::-1, WIN - 1::-1]
                        grid = "p (i j) -> p i j"
                        last = dve.tensor_tensor(bias_mask[:, pair, w, :].rearrange(grid, j=WIN), seen,
                                                 mask_in[:, w, :].rearrange(grid, j=WIN), ALU.add)
                last.then_inc(bias_ready, 1)
                dve.wait_ge(bias_ready, 1)

            def group_stats(layer, img, src):
                s, done = stat[layer], gn_small[layer]
                reach(dve, done, previous(img), GN_STEPS)
                for g in range(G):
                    dve.bn_stats(s[:, 6 * g:6 * g + 6], src[:, g * TOK:(g + 1) * TOK]).then_inc(done, 1)
                mean, sq_sum = s[:, 1:12:3], s[:, 2:12:3]
                reach(dve, done, img, GN_STEPS, 2)
                dve.tensor_tensor(s[:, 12:16], mean, mean, ALU.mult).then_inc(done, 1)
                reach(dve, done, img, GN_STEPS, 3)
                dve.scalar_tensor_tensor(sq_sum, sq_sum, 2.0 / TOK, s[:, 12:16], ALU.mult, ALU.add).then_inc(done, 1)

            def group_var(layer, img):
                s, done = stat[layer], gn_small[layer]
                reach(dve, gn_sum[layer], img)
                means = ps[:, GM_BANK[layer], 0:6].rearrange("p (g v) -> p g v", v=3)
                dve.tensor_copy(s[:, 20:24].rearrange("p (g v) -> p g v", v=2), means[:, :, 1:3]).then_inc(done, 1)
                reach(dve, done, img, GN_STEPS, 5)
                dve.tensor_tensor(s[:, 24:26], s[:, 20:24:2], s[:, 20:24:2], ALU.mult).then_inc(done, 1)
                reach(dve, done, img, GN_STEPS, 6)
                dve.tensor_tensor(s[:, 30:32], s[:, 21:24:2], s[:, 24:26], ALU.subtract).then_inc(done, 1)
                reach(dve, done, img, GN_STEPS, 7)
                dve.tensor_scalar(s[:, 26:28], s[:, 30:32], 0.0, GN_EPS, ALU.max, ALU.add).then_inc(done, 1)

            def group_norm(layer, img, src):
                s, done = stat[layer], gn_small[layer]
                reach(dve, gn_pow[layer], img)
                reach(dve, xn_lo[layer], previous(img))
                for g in range(G):
                    cols = slice(g * TOK, (g + 1) * TOK)
                    dve.tensor_scalar(xn32[layer][:, cols], src[:, cols], s[:, 20 + 2 * g:21 + 2 * g],
                                      s[:, 28 + g:29 + g], ALU.subtract, ALU.mult).then_inc(done, 1)

            def turn(a, img):
                reach(dve, kv1_proj[a], img)
                reach(dve, kv_lo[1 - a], img if a else previous(img))
                src = ps[:, KV_BANK[a]:KV_BANK[a] + 2, :].rearrange("p t (g r c) -> p (t g) r c", r=SIDE, c=SIDE)
                if a == 0:
                    src = src.rearrange("p h r c -> p h c r")
                dst = kv32[:].rearrange("p t (g s i) -> p (t g) s i", s=SEQ, i=SEQ)
                dve.transpose(dst, src).then_inc(kv_turned[a], 1)

            def widen_kv(a, img):
                reach(dve, kv_lo[a], img)
                reach(dve, gram_done[a], previous(img))
                src = kv[a][:].rearrange("p t h (s e) -> p t (h s) e", e=32)
                k_dst = k_wide[a][:].rearrange("p t s q e -> p (t s) q e")
                v_dst = v_wide[a][:].rearrange("p t s q e -> p (t s) q e")
                for q in range(4):
                    dve.tensor_scalar(k_dst[:, :, q, :], src[:, 0], quad_mask[:, q:q + 1], None, ALU.mult)
                for q in range(2):
                    last = dve.tensor_scalar(v_dst[:, :, q, :], src[:, 1], odd_mask[:, q:q + 1], None, ALU.mult)
                last.then_inc(kv_widened[a], 1)

            def gram_sum(a, img):
                reach(dve, gram_even[a], img)
                reach(dve, gram_lo[1 - a], img if a else previous(img))
                v = ps[:, G_BANK[a]:G_BANK[a] + 2, :].rearrange("p b (s h e) -> p (b s) h e", h=2, e=DH)
                flat = "p (s e) -> p s e"
                dve.scalar_tensor_tensor(gram32[:].rearrange(flat, e=DH), v[:, :, 1, :], odd_mask_g[:, 1:2],
                                         gram_t[:].rearrange(flat, e=DH), ALU.mult,
                                         ALU.add).then_inc(gram_summed[a], 1)

            def widen_gram(a, img):
                reach(dve, gram_lo[a], img)
                reach(dve, o1_done[a], previous(img))
                src = gram[a][:].rearrange("p t (s e) -> p (t s) e", e=DH)
                dst = gram_wide[a][:].rearrange("p t s h e -> p (t s) h e")
                for h in range(ACT_HEADS, 8):
                    last = dve.tensor_scalar(dst[:, :, h, :], src, head_mask[:, h:h + 1], None, ALU.mult)
                last.then_inc(widened_dve[a], 1)

            def o1_sum(a, img):
                reach(dve, o1_aside[a], img)
                both = ps[:, O_BANK[a]:O_BANK[a] + 2, :].rearrange("p b (s t i) -> p (b s) t i", t=2, i=SEQ)
                whole = o1_32[a][:].rearrange("p (s i) -> p s i", i=SEQ)
                dve.tensor_tensor(whole, both[:, :, 0, :], whole, ALU.add).then_inc(o1_summed[a], 1)

            def spread_v(img):
                if is_first(img):
                    dve.wait_ge(late_in, 16 * 5)
                reach(dve, v_proj, img)
                reach(dve, pv_done, previous(img))
                for half in range(2):
                    rows = slice(64 * half, 64 * half + 64)
                    src = ps[rows, V_BANK, :].rearrange("p (a b d) -> p a b d", b=2, d=DH)
                    add = bv_rows[rows].rearrange("p t (a b d) -> p (t a) b d", b=2, d=DH)
                    for b in range(2):
                        dst = v_diag[64 * b:64 * b + 64, half].rearrange("p t a d -> p (t a) d")
                        last = dve.scalar_tensor_tensor(dst[:, :, DH * b:DH * b + DH], src[:, :, b, :], 1.0 / WS,
                                                        add[:, :, b, :], ALU.mult, ALU.add)
                last.then_inc(v_ready, 1)

            def scale_qk(img):
                if is_first(img):
                    axial_weights_low()
                    bias_tables()
                    dve.wait_ge(tables_ready, 1)
                reach(dve, rnorm_done, img)
                reach(dve, qk_lo, previous(img))
                for g in range(G):
                    cols = slice(g * TOK, (g + 1) * TOK)
                    dve.scalar_tensor_tensor(qk32[:, 0, cols], qk_sq[:, 0, cols], q_cap[:, g:g + 1],
                                             ps[:, QK_BANK, cols], ALU.min, ALU.mult)
                dve.scalar_tensor_tensor(qk32[:, 1, :], qk_sq[:, 1, :], 8.0 / (QS * NORM_MIN),
                                         ps[:, QK_BANK + 1, :], ALU.min, ALU.mult).then_inc(qk_scaled, 1)

            def mask_k(img):
                reach(dve, qk_lo, img)
                for g in range(G):
                    reach(dve, scores_done[g], previous(img))
                src = qk[:, :, 1].rearrange("p t g n -> p t (g n)").rearrange("p t (s n) -> p t s n", n=N)
                dst = k_heads[:].rearrange("p t g w h n -> p t (g w) h n")
                for h in range(8):
                    last = dve.tensor_scalar(dst[:, :, :, h, :], src, head_mask[:, h:h + 1], None, ALU.mult)
                last.then_inc(k_masked, 1)

            def add_bias(g, img):
                reach(dve, scores_done[g], img)
                reach(dve, den_done, previous(img))
                reach(dve, pv_done, previous(img))
                dve.tensor_tensor(probs[:, 4 * g:4 * g + 4, :].rearrange("p a n -> p (a n)"),
                                  ps[:, S_BANK[g]:S_BANK[g] + 2, :].rearrange("p b n -> p (b n)"),
                                  bias_mask[:, 4 * g:4 * g + 4].rearrange("p a w n -> p (a w n)"),
                                  ALU.add).then_inc(biased[g], 1)

            def invert_den(img):
                reach(dve, den_done, img)
                reach(dve, o_scaled, previous(img))
                dve.reciprocal(den_inv[:], ps[:, DEN_BANK, :]).then_inc(den_inverted, 1)

            def scale_o(img):
                reach(dve, den_inverted, img)
                reach(dve, pv_done, img)
                reach(dve, o_lo, previous(img))
                dve.tensor_tensor(o32[:], ps[:, PV_BANK, :], den_inv[:], ALU.mult).then_inc(o_scaled, 1)

            def add_x(img):
                reach(dve, z_ready, img)
                reach(dve, y_added, earlier(img, 2))
                dst = x1[:, img.par].rearrange("p (a i b j) -> p a i b j", i=WIN, b=2, j=WIN)
                for b in range(2):
                    last = dve.tensor_tensor(dst[:, :, :, b, :], windows(z[:])[:, :, b],
                                             windows(x_t[:, img.par])[:, :, b], ALU.add)
                last.then_inc(x1_ready, 1)

            def group_stats0(img):
                reach(dve, xt_copied, img)
                group_stats(0, img, x_t[:, img.par])

            def group_stats1(img):
                reach(dve, x1_ready, img)
                group_stats(1, img, x1[:, img.par])

            def add_x1(img):
                reach(dve, y_proj, img)
                reach(dve, yt_done, previous(img))
                src, add, dst = raster(ps[:, Y_BANK, :]), raster(x1[:, img.par]), raster(y[:])
                edge = SIDE - SHIFT
                dve.scalar_tensor_tensor(dst[:, :, SHIFT:], src[:, :, :edge], 1.0 / (WS * WS), add[:, :, :edge],
                                         ALU.mult, ALU.add)
                dve.scalar_tensor_tensor(dst[:, :, :SHIFT], src[:, :, edge:], 1.0 / (WS * WS), add[:, :, edge:],
                                         ALU.mult, ALU.add).then_inc(y_added, 1)

            def step(i, c):
                for img in there(i, c - 3):
                    turn(0, img)
                for img in there(i, c - 2):
                    add_bias(0, img)
                for img in there(i, c - 4):
                    widen_gram(1, img)
                for img in there(i, c - 3):
                    turn(1, img)
                    widen_kv(0, img)
                for img in there(i, c - 4):
                    o1_sum(1, img)
                for img in there(i, c - 2):
                    invert_den(img)
                for img in there(i, c - 3):
                    gram_sum(0, img)
                for img in there(i, c - 2):
                    scale_o(img)
                for img in there(i, c - 1):
                    scale_qk(img)
                for img in there(i, c - 3):
                    widen_kv(1, img)
                    widen_gram(0, img)
                for img in there(i, c - 4):
                    add_x1(img)
                for img in there(i, c - 1):
                    mask_k(img)
                for img in there(i, c - 2):
                    add_x(img)
                    group_stats1(img)
                for img in there(i, c - 3):
                    gram_sum(1, img)
                for img in there(i, c - 2):
                    group_var(1, img)
                for img in there(i, c - 1):
                    add_bias(1, img)
                for img in there(i, c - 2):
                    group_norm(1, img, x1[:, img.par])
                for img in there(i, c):
                    group_stats0(img)
                for img in there(i, c - 1):
                    spread_v(img)
                for img in there(i, c):
                    group_var(0, img)
                for img in there(i, c - 3):
                    o1_sum(0, img)
                for img in there(i, c):
                    group_norm(0, img, x_t[:, img.par])

            over_steps(dve, step)


_INS = ["x", "L0_conv_Wq", "L0_conv_Wk", "L0_conv_Wv", "L0_conv_bv", "L0_conv_Wo", "L0_conv_bo",
        "L0_conv_logit_scale", "L0_conv_cpb_w1", "L0_conv_cpb_b1", "L0_conv_cpb_w2",
        "L1_conv_w_qkv0", "L1_conv_w_out0", "L1_conv_w_qkv1", "L1_conv_w_out1"]


def kernel(**inputs):
    import concourse.bacc as bacc
    from concourse.bass_utils import run_bass_kernel_spmd

    nc = bacc.Bacc("TRN2", target_bir_lowering=False, num_devices=1)
    arrays = {name: np.ascontiguousarray(inputs[name]) for name in _INS} | constants()
    args = [nc.dram_tensor(name, a.shape, mybir.dt.from_np(a.dtype), kind="ExternalInput").ap()
            for name, a in arrays.items()]
    out = nc.dram_tensor("out", (IMAGES, SIDE, SIDE, D), F32, kind="ExternalOutput").ap()
    scratch = nc.dram_tensor("position_table", (HEADS, REL * REL), F32, kind="Internal").ap()
    build(nc, *args, out, scratch)
    r = run_bass_kernel_spmd(nc, [arrays], core_ids=[0])
    return r.results[0]["out"]
```
